# Optimizing a Trainium2 kernel written in Bass

```python
import numpy as np
import jax
import jax.numpy as jnp

def _softmax(x, axis=-1):
    return jax.nn.softmax(x, axis=axis)

def _gelu(x):
    return jax.nn.gelu(x, approximate=True)

def _silu(x):
    return jax.nn.silu(x)

def _sigmoid(x):
    return jax.nn.sigmoid(x)

def _layernorm(x, axis=-1, eps=1e-05):
    m = jnp.mean(x, axis=axis, keepdims=True)
    v = jnp.var(x, axis=axis, keepdims=True)
    return (x - m) / jnp.sqrt(v + eps)

def _scatter_add(tgt, idx, src, axis=0):
    return tgt.at[idx].add(src)

def _segment_sum(src, seg, n):
    return jax.ops.segment_sum(src, seg, n)
kernel_name = 'mk_adj_ffn_d2_adj_r2_0553c4'

def setup_inputs(seed: int=0):
    np.random.seed(seed)
    _w = jnp.asarray

    def _rec_inputs():
        import jax
        import jax.numpy as jnp
        _gk = jax.random.key(seed)
        x = -0.0002928 + 1 * jax.random.normal(jax.random.fold_in(_gk, 1), (16, 512, 128), jnp.float32)
        _w = (1.0 + jnp.arange(512, dtype=jnp.float32)) ** (-0.5)
        _w = _w / _w.mean()
        _pij = jnp.clip(0.03125 * _w[:, None] * _w[None, :], 0.0, 1.0)
        _a = jax.random.uniform(jax.random.fold_in(_gk, 2), (16, 512, 512)) < _pij
        adj = _a.astype(jnp.int32)
        return (x, adj)
    x, adj = _rec_inputs()

    def _L0_gnn_setup():
        import jax, jax.numpy as jnp
        import numpy as np
        key = jax.random.key(seed)
        k1, k2, k3, k4 = jax.random.split(key, 4)
        B, N, F, U = (8, 1024, 128, 128)
        x = jax.random.normal(k1, (B, N, F), dtype=jnp.float32)
        adj = jax.random.randint(k2, (B, N, N), 0, 2, dtype=jnp.int32)
        W_msg = jax.random.normal(k3, (F, U), dtype=jnp.float32) / np.sqrt(F)
        W_upd = jax.random.normal(k4, (F, U), dtype=jnp.float32) / np.sqrt(F)
        bias = jnp.zeros((U,), dtype=jnp.float32)
        return {'x': x, 'adj': adj, 'W_msg': W_msg, 'W_upd': W_upd, 'bias': bias}
    _L0_gnn_all = _L0_gnn_setup()
    _L0_gnn_in = {k: v for k, v in _L0_gnn_all.items() if k in ('W_msg', 'W_upd', 'bias')}
    del _L0_gnn_all

    def _L0_ffn_setup():
        import jax, jax.numpy as jnp
        import numpy as np
        TOP_K = 2
        LN_EPS = 1e-05
        key = jax.random.key(seed)
        ks = jax.random.split(key, 8)
        B, S, D, E, H = (16, 512, 128, 8, 512)
        x = jax.random.normal(ks[0], (B, S, D), dtype=jnp.float32)
        Wr = jax.random.normal(ks[1], (D, E), dtype=jnp.float32) * 0.1
        br = jnp.zeros((E,), dtype=jnp.float32)
        ln_g = jnp.ones((E, D), dtype=jnp.float32)
        ln_b = jnp.zeros((E, D), dtype=jnp.float32)
        W1 = jax.random.normal(ks[2], (E, D, H), dtype=jnp.float32) * (1.0 / np.sqrt(D))
        b1 = jnp.zeros((E, H), dtype=jnp.float32)
        W2 = jax.random.normal(ks[3], (E, H, D), dtype=jnp.float32) * (1.0 / np.sqrt(H))
        b2 = jnp.zeros((E, D), dtype=jnp.float32)
        return {'x': x, 'Wr': Wr, 'br': br, 'ln_g': ln_g, 'ln_b': ln_b, 'W1': W1, 'b1': b1, 'W2': W2, 'b2': b2}
    _L0_ffn_all = _L0_ffn_setup()
    _L0_ffn_in = {k: v for k, v in _L0_ffn_all.items() if k in ('Wr', 'br', 'ln_g', 'ln_b', 'W1', 'b1', 'W2', 'b2')}
    del _L0_ffn_all

    def _L1_gnn_setup():
        import jax, jax.numpy as jnp
        import numpy as np
        NEG_BIG = -9000000000000000.0
        LEAKY_SLOPE = 0.2
        key = jax.random.key(seed)
        k1, k2, k3, k4 = jax.random.split(key, 4)
        B, N, F_in, F_out = (8, 1024, 128, 128)
        h = jax.random.normal(k1, (B, N, F_in), dtype=jnp.float32)
        adj = jax.random.randint(k2, (B, N, N), 0, 2, dtype=jnp.int32)
        W = jax.random.normal(k3, (F_out, F_in), dtype=jnp.float32) * (1.414 * (6.0 / (F_in + F_out)) ** 0.5)
        a = jax.random.normal(k4, (2 * F_out, 1), dtype=jnp.float32) * 0.1
        return {'h': h, 'adj': adj, 'W': W, 'a': a}
    _L1_gnn_all = _L1_gnn_setup()
    _L1_gnn_in = {k: v for k, v in _L1_gnn_all.items() if k in ('W', 'a')}
    del _L1_gnn_all

    def _L1_ffn_setup():
        import jax, jax.numpy as jnp
        import numpy as np
        B, S, D, E, H, K = (4, 2048, 128, 8, 256, 2)
        key = jax.random.key(seed)
        ks = jax.random.split(key, 6)
        x = jax.random.normal(ks[0], (B, S, D), jnp.float32)
        Wg = jax.random.normal(ks[1], (D, E), jnp.float32) * 0.02
        bg = jnp.zeros((E,), jnp.float32)
        W1 = jax.random.normal(ks[2], (E, D, H), jnp.float32) * 0.02
        b1 = jnp.zeros((E, H), jnp.float32)
        W2 = jax.random.normal(ks[3], (E, H, D), jnp.float32) * 0.02
        b2 = jnp.zeros((E, D), jnp.float32)
        return {'x': x, 'Wg': Wg, 'bg': bg, 'W1': W1, 'b1': b1, 'W2': W2, 'b2': b2}
    _L1_ffn_all = _L1_ffn_setup()
    _L1_ffn_in = {k: v for k, v in _L1_ffn_all.items() if k in ('Wg', 'bg', 'W1', 'b1', 'W2', 'b2')}
    del _L1_ffn_all
    return {'x': x, 'adj': adj, 'L0_gnn_W_msg': _L0_gnn_in['W_msg'], 'L0_gnn_W_upd': _L0_gnn_in['W_upd'], 'L0_gnn_bias': _L0_gnn_in['bias'], 'L0_ffn_Wr': _L0_ffn_in['Wr'], 'L0_ffn_br': _L0_ffn_in['br'], 'L0_ffn_ln_g': _L0_ffn_in['ln_g'], 'L0_ffn_ln_b': _L0_ffn_in['ln_b'], 'L0_ffn_W1': _L0_ffn_in['W1'], 'L0_ffn_b1': _L0_ffn_in['b1'], 'L0_ffn_W2': _L0_ffn_in['W2'], 'L0_ffn_b2': _L0_ffn_in['b2'], 'L1_gnn_W': _L1_gnn_in['W'], 'L1_gnn_a': _L1_gnn_in['a'], 'L1_ffn_Wg': _L1_ffn_in['Wg'], 'L1_ffn_bg': _L1_ffn_in['bg'], 'L1_ffn_W1': _L1_ffn_in['W1'], 'L1_ffn_b1': _L1_ffn_in['b1'], 'L1_ffn_W2': _L1_ffn_in['W2'], 'L1_ffn_b2': _L1_ffn_in['b2']}

def reference(x, adj, L0_gnn_W_msg, L0_gnn_W_upd, L0_gnn_bias, L0_ffn_Wr, L0_ffn_br, L0_ffn_ln_g, L0_ffn_ln_b, L0_ffn_W1, L0_ffn_b1, L0_ffn_W2, L0_ffn_b2, L1_gnn_W, L1_gnn_a, L1_ffn_Wg, L1_ffn_bg, L1_ffn_W1, L1_ffn_b1, L1_ffn_W2, L1_ffn_b2):
    import jax
    import jax.numpy as jnp

    def _L0_gnn_ref(x, adj, W_msg, W_upd, bias):
        import jax, jax.numpy as jnp
        import numpy as np
        a = adj.astype(x.dtype)
        h = jnp.einsum('bnf,fu->bnu', x, W_msg)
        msg_sum = jnp.einsum('bij,biu->bju', a, h)
        deg = jnp.sum(a, axis=1)
        messages = jnp.where(deg[..., None] > 0, msg_sum / jnp.maximum(deg, 1.0)[..., None], 0.0)
        out = jnp.einsum('bnf,fu->bnu', x, W_upd) + messages + bias
        return jax.nn.relu(out)

    def _L0_ffn_ref(x, Wr, br, ln_g, ln_b, W1, b1, W2, b2):
        import jax, jax.numpy as jnp
        import numpy as np
        TOP_K = 2
        LN_EPS = 1e-05
        B, S, D = x.shape
        N = B * S
        xt = x.reshape(N, D)
        logits = xt @ Wr + br
        probs = jax.nn.softmax(logits, axis=-1)
        top_p, top_idx = jax.lax.top_k(probs, TOP_K)
        weights = top_p / top_p.sum(axis=-1, keepdims=True)
        mu = xt.mean(axis=-1, keepdims=True)
        var = ((xt - mu) ** 2).mean(axis=-1, keepdims=True)
        xn = (xt - mu) * jax.lax.rsqrt(var + LN_EPS)
        xe = xn[None, :, :] * ln_g[:, None, :] + ln_b[:, None, :]
        h = jax.nn.gelu(jnp.einsum('end,edh->enh', xe, W1) + b1[:, None, :], approximate=False)
        y = jnp.einsum('enh,ehd->end', h, W2) + b2[:, None, :]
        y_tok = jnp.transpose(y, (1, 0, 2))
        sel = jnp.take_along_axis(y_tok, top_idx[:, :, None], axis=1)
        out = (weights[:, :, None] * sel).sum(axis=1)
        return out.reshape(B, S, D)

    def _L1_gnn_ref(h, adj, W, a):
        import jax, jax.numpy as jnp
        import numpy as np
        NEG_BIG = -9000000000000000.0
        LEAKY_SLOPE = 0.2
        Wh = jnp.einsum('bnf,of->bno', h, W)
        F_out = W.shape[0]
        a1 = a[:F_out, 0]
        a2 = a[F_out:, 0]
        s1 = Wh @ a1
        s2 = Wh @ a2
        e = s1[:, :, None] + s2[:, None, :]
        e = jax.nn.leaky_relu(e, negative_slope=LEAKY_SLOPE)
        e = jnp.where(adj == 0, NEG_BIG, e)
        attention = jax.nn.softmax(e, axis=-1)
        h_prime = jnp.einsum('bij,bjf->bif', attention, Wh)
        return jax.nn.elu(h_prime)

    def _L1_ffn_ref(x, Wg, bg, W1, b1, W2, b2):
        import jax, jax.numpy as jnp
        import numpy as np
        B, S, D, E, H, K = (4, 2048, 128, 8, 256, 2)
        Bv, Sv, Dv = x.shape
        gate_scores = x @ Wg + bg
        _, idx = jax.lax.top_k(gate_scores, K)
        mask = jax.nn.one_hot(idx, E, dtype=x.dtype).sum(axis=-2)
        xf = x.reshape(-1, Dv)
        mf = mask.reshape(-1, E)
        h = jax.nn.gelu(jnp.einsum('td,edh->teh', xf, W1) + b1[None], approximate=False)
        y = jnp.einsum('teh,ehd->ted', h, W2) + b2[None]
        out = jnp.einsum('ted,te->td', y, mf)
        return out.reshape(Bv, Sv, Dv)
    x = x + _L0_gnn_ref(_layernorm(x, axis=-1), adj, L0_gnn_W_msg, L0_gnn_W_upd, L0_gnn_bias)
    x = x + _L0_ffn_ref(_layernorm(x, axis=-1), L0_ffn_Wr, L0_ffn_br, L0_ffn_ln_g, L0_ffn_ln_b, L0_ffn_W1, L0_ffn_b1, L0_ffn_W2, L0_ffn_b2)
    x = x + _L1_gnn_ref(_layernorm(x, axis=-1), adj, L1_gnn_W, L1_gnn_a)
    x = x + _L1_ffn_ref(_layernorm(x, axis=-1), L1_ffn_Wg, L1_ffn_bg, L1_ffn_W1, L1_ffn_b1, L1_ffn_W2, L1_ffn_b2)
    return x

_drawn_inputs = setup_inputs


def setup_inputs(seed=0):
    import zlib

    import numpy as np

    out = dict(_drawn_inputs(seed))
    spreads = {'L0_gnn_bias': (0.0, 0.1),
     'L0_ffn_br': (0.0, 0.1),
     'L0_ffn_ln_g': (1.0, 0.2),
     'L0_ffn_ln_b': (0.0, 0.1),
     'L0_ffn_b1': (0.0, 0.1),
     'L0_ffn_b2': (0.0, 0.1),
     'L1_ffn_bg': (0.0, 0.1),
     'L1_ffn_b1': (0.0, 0.589),
     'L1_ffn_b2': (0.0, 0.1)}
    factors = {}
    for name, (base, spread) in spreads.items():
        noise = np.random.default_rng([zlib.crc32(name.encode()), seed]).standard_normal(out[name].shape)
        drawn = base * np.exp(spread * noise) if base else spread * noise
        out[name] = jnp.asarray(drawn.astype(out[name].dtype))
    for name, factor in factors.items():
        out[name] = (out[name] * factor).astype(out[name].dtype)
    return out
```

```python
import numpy as np
import concourse.bass as bass
from concourse import mybir
from contextlib import ExitStack

P = 128
NB, N, D = 16, 512, 128
T = N // P
NT = NB * T
E = 8
H0, H1 = 512, 256
EPS = 1e-5
SLOPE = 0.2
NEG = -float(2 ** 53)
WS = 64.0

F32, F16, BF16 = mybir.dt.float32, mybir.dt.float16, mybir.dt.bfloat16
I32, U32 = mybir.dt.int32, mybir.dt.uint32
ALU = mybir.AluOpType
ACT = mybir.ActivationFunctionType
AX = mybir.AxisListType


class Chain:

    def __init__(self, eng, sem):
        self.eng, self.sem, self.base, self.k = eng, sem, 0, 0

    def __call__(self, ins, alone=None):
        self.k += 1
        ins.then_inc(self.sem, 1)
        if alone:
            alone(self.eng, (self.sem, self.base + self.k))
        else:
            self.eng.wait_ge(self.sem, self.base + self.k)

    def start(self, base):
        self.base, self.k = base, 0


def build(nc, x, adj, W_msg, W_upd, g_bias, Wr, br, ln_g, ln_b, W1a, b1a, W2a, b2a,
          W, a, Wg, bg, W1b, b1b, W2b, b2b, identf, identh, sel, iota8, out):
    ctx = ExitStack()
    with ctx:
        def sb(name, shape, dt=F32):
            return ctx.enter_context(nc.sbuf_tensor(name, shape, dt))

        def sem(name):
            return ctx.enter_context(nc.semaphore(name))

        xs = sb("xs", [P, NT * D])
        mv = sb("mv", [P, NT * 2])
        rs = sb("rs", [P, NT])
        ps = ctx.enter_context(nc.psum_tensor("ps", [P, 8, 512], F32))
        idf = sb("idf", [P, P])
        idh = sb("idh", [P, P], F16)
        selh = sb("selh", [16, E * P], F16)
        io8 = sb("io8", [P, T * E])
        epsv = sb("epsv", [P, NT])
        mhalf = sb("mhalf", [P, NT])

        stage = sb("stage", [P, 8192])
        wA = [sb(f"wA{k}", [P, 2 * D], F16) for k in range(2)]
        wC = [sb(f"wC{k}", [P, D + 2], F16) for k in range(2)]
        wS = [sb(f"wS{k}", [P, P], F16) for k in range(2)]
        wR = [[sb(f"wR{l}{k}", [P, E], F16) for k in range(2)] for l in range(2)]
        w1 = [[sb(f"w1{l}{k}", [P, E * h], F16) for k in range(2)] for l, h in enumerate((H0, H1))]
        w2 = [[sb(f"w2{l}{k}", [P, E * h], F16) for k in range(2)] for l, h in enumerate((H0, H1))]
        b1 = [sb(f"b1{l}", [P, E * h // P]) for l, h in enumerate((H0, H1))]
        b2 = [[sb(f"b2{l}{k}", [16, D], F16) for k in range(2)] for l in range(2)]
        gb = sb("gb", [P, T * D])
        rb = [sb(f"rb{l}", [P, T * E]) for l in range(2)]
        gT = sb("gT", [P, E])
        bT = sb("bT", [P, E])
        acol = sb("acol", [P, 2])
        smf = sb("smf", [P, 2 * D + 8])
        b2f = sb("b2f", [16, 2 * D])
        zt = sb("zt", [P, 64])
        cells = iter(range(64))

        s_w = sem("s_w")
        s_c = sem("s_c")
        s_x = sem("s_x")
        s_ch = sem("s_ch")
        s_pc = sem("s_pc")
        s_setup_pe = sem("s_setup_pe")
        s_stage_free = sem("s_stage_free")
        s_ready = sem("s_ready")
        s_eps = sem("s_eps")
        s_always = sem("s_always")
        s_st = [sem(f"s_st{k}") for k in range(4)]
        s_rs = [sem(f"s_rs{k}") for k in range(4)]

        block_ctx = nc.Block()
        block = ctx.enter_context(block_ctx)

        def bank(k):
            return ps[:, k, :]

        adjI = [sb(f"adjI{j}", [P, T * N], I32) for j in range(2)]
        adjF = [sb(f"adjF{j}", [P, T * N], F16) for j in range(2)]
        xn = [sb(f"xn{j}", [P, T * D]) for j in range(2)]
        xTh = [sb(f"xTh{j}", [P, N], F16) for j in range(2)]
        xTl = [sb(f"xTl{j}", [P, N], F16) for j in range(2)]
        h32 = [sb(f"h32{k}", [P, 4 * N]) for k in range(2)]
        upd = [h32[0][:, j * T * D:(j + 1) * T * D] for j in range(2)]
        hh = [h32[1][:, 0:1024].bitcast(F16)[:, j * T * (D + 1):(j + 1) * T * (D + 1)] for j in range(2)]
        hl = [h32[1][:, 1024:2048].bitcast(F16)[:, j * T * D:(j + 1) * T * D] for j in range(2)]
        deg = [sb(f"deg{j}", [P, 2 * T]) for j in range(2)]
        st6 = sb("st6", [P, T * 6])
        agg8 = sb("agg8", [P, T * 2])

        def sems(prefix, names):
            return {n: sem(f"{prefix}_{n}") for n in names}

        A = sems("A", ["adj0", "adj1", "xload0", "xload1", "conv", "xn", "tr", "hi", "lo", "proj", "hh", "hl", "upd", "agg",
                       "ch", "read", "fin"])
        C = sems("C", ["adj0", "adj1", "conv", "xn", "tr", "hi", "lo", "proj", "wh", "bias", "e", "p", "ptr", "pt",
                       "av", "mn", "ex", "ch", "fin"])
        FF = [sems(f"F{l}", ["xn", "tr", "hi", "lo", "lg", "rt", "wt", "wtc", "up", "gelu", "hhi", "hlo", "y", "wb",
                             "wbc", "comb", "fin", "xadd", "ch", "th", "d"]) for l in range(2)]

        def mark(eng):
            c = next(cells)
            return eng.memset(zt[:, c:c + 1], 0.0)

        def wait_alone(eng, *pairs):
            pairs = [(semaphore, v if isinstance(v, int) else eng.to_reg(v)) for semaphore, v in pairs]
            eng.wait_ge(s_always, 1)
            for semaphore, v in pairs:
                eng.wait_ge(semaphore, v)

        def aggregate(chain, b, dst):
            for t in range(T):
                last = nc.vector.bn_aggr(agg8[:, 2 * t:2 * t + 2], st6[:, 6 * t:6 * t + 6])
            chain(last, wait_alone)
            return nc.vector.tensor_copy(dst[:, bass.ds(b * (T * 2), T * 2)], agg8[:, :])

        def normalise(dve, b, j):
            for t in range(T):
                last = nc.vector.tensor_scalar(
                    xn[j][:, t * D:(t + 1) * D], xs[:, bass.ds(b * (T * D) + t * D, D)],
                    mv[:, bass.ds(b * (T * 2) + 2 * t, 1)], rs[:, bass.ds(b * T + t, 1)],
                    ALU.subtract, ALU.mult)
            return last

        def transpose_tiles(pe, dst, src):
            for t in range(T):
                last = nc.tensor.transpose(dst[:, t * P:(t + 1) * P], src[:, t * D:(t + 1) * D], idf[:, :])
            return last

        def pool_rstd(pool, which, twice):
            mvv = mv[:, :].rearrange("p (n two) -> p n two", two=2)
            pool.wait_ge(s_st[which], NB if which else 1)
            n = [0]

            def link(ins):
                n[0] += 1
                pool_base[0] += 1
                ins.then_inc(s_pc, 1)
                pool.wait_ge(s_pc, pool_base[0])

            link(nc.gpsimd.tensor_tensor(rs[:, :], mvv[:, :, 1], epsv[:, :], ALU.add))
            if not twice:
                nc.gpsimd.tensor_tensor(rs[:, :], rs[:, :], mhalf[:, :], ALU.pow).then_inc(s_rs[which], 1)
                return
            link(nc.gpsimd.tensor_tensor(rs[:, :], rs[:, :], mhalf[:, :], ALU.pow))
            link(nc.gpsimd.tensor_tensor(cinv[:, :], rs[:, :], rs[:, :], ALU.mult))
            link(nc.gpsimd.tensor_tensor(cinv[:, :], cinv[:, :], mvv[:, :, 1], ALU.mult))
            link(nc.gpsimd.tensor_tensor(cinv[:, :], cinv[:, :], epsv[:, :], ALU.add))
            link(nc.gpsimd.tensor_tensor(ctmp[:, :], cinv[:, :], mhalf[:, :], ALU.pow))
            link(nc.gpsimd.tensor_tensor(cinv[:, :], cinv[:, :], ctmp[:, :], ALU.mult))
            nc.gpsimd.tensor_tensor(rs[:, :], rs[:, :], ctmp[:, :], ALU.mult).then_inc(s_rs[which], 1)

        pool_base = [0]
        cinv = sb("cinv", [P, NT])
        ctmp = sb("ctmp", [P, NT])

        hhi = [sb(f"hhi{k}", [P, 4 * N], F16) for k in range(2)]
        hlo = [sb(f"hlo{k}", [P, 4 * N], F16) for k in range(2)]
        wbs = [sb(f"wbs{k}", [P, N]) for k in range(2)]
        tmpy = sb("tmpy", [P, N])
        acc = [sb(f"acc{k}", [P, N]) for k in range(2)]
        mv3 = sb("mv3", [P, NT * 2])
        lg = sb("lg", [P, T * E])
        mx8 = sb("mx8", [P, T * E])
        ix8 = sb("ix8", [P, T * E], U32)
        ixf = sb("ixf", [P, T * E])
        oh = sb("oh", [P, 2 * T * E])
        ws = sb("ws", [P, 4 * T])
        w16 = sb("w16", [P, T * 16], F16)
        wT = [sb(f"wT{k}", [16, N], F16) for k in range(2)]

        def v3(ap, k):
            return ap.rearrange("p (t k) -> p t k", k=k)

        def whE(j):
            return acc_w[j][:, :].rearrange("p (t d) -> p t d", d=D + 1)

        acc_w = [sb(f"whE{k}", [P, T * (D + 1)]) for k in range(2)]

        def tt(j, t):
            return h32[j][:, t * N:(t + 1) * N]

        def eA(t):
            return stage[:, (t % 2) * N:(t % 2) * N + N]

        def eB(t):
            return stage[:, 1024 + (t % 2) * N:1024 + (t % 2) * N + N]

        def pm(t):
            return stage[:, 2048 + (t % 2) * N:2048 + (t % 2) * N + N]

        def PT(t):
            return stage[:, 3072 + (t % 2) * N:3072 + (t % 2) * N + N]

        def mnb(j):
            return stage[:, 4096:4096 + N]

        def hpb(j):
            return stage[:, 4608:4608 + N]

        rowb = sb("rowb", [P, 2 * 8 * T])

        def bi(j, k, t):
            o = j * 8 * T + k * T + t
            return rowb[:, o:o + 1]

        def copy_pt(act, b, t):
            q = 4 * b + t
            act.wait_ge(C["ptr"], q + 1)
            act.wait_ge(C["av"], q + 7)
            nc.scalar.activation(PT(t), bank(4 + t % 2), ACT.Copy).then_inc(C["pt"], 1)

        @block.sync
        def _(sp):
            sp.dma_start(idf[:, :], identf).then_inc(s_c, 16)
            sp.dma_start(idh[:, :], identh).then_inc(s_c, 16)
            sp.dma_start(selh[:, :], sel).then_inc(s_c, 16)
            sp.dma_start(io8[:, :], iota8).then_inc(s_c, 16)
            sp.dma_start(smf[:, 0:D], W_msg).then_inc(s_c, 16)
            sp.dma_start(smf[:, D:2 * D], W_upd).then_inc(s_c, 16)
            sp.dma_start(gT[:, :], ln_g.rearrange("e d -> d e"), allow_slow_non_contiguous=True).then_inc(s_c, 16)
            sp.dma_start(bT[:, :], ln_b.rearrange("e d -> d e"), allow_slow_non_contiguous=True).then_inc(s_c, 16)
            sp.dma_start(acol[:, :], a.rearrange("(k o) one -> o (k one)", k=2), allow_slow_non_contiguous=True).then_inc(s_c, 16)
            for k in range(2):
                sp.dma_start(b2f[8 * k:8 * k + 8, 0:D], b2a).then_inc(s_c, 16)
                sp.dma_start(b2f[8 * k:8 * k + 8, D:2 * D], b2b).then_inc(s_c, 16)
            sp.dma_start(b1[1][:, :], b1b.rearrange("e (c p) -> p (e c)", p=P), allow_slow_non_contiguous=True).then_inc(s_c, 16)
            sp.dma_start(b1[0][:, :], b1a.rearrange("e (c p) -> p (e c)", p=P), allow_slow_non_contiguous=True).then_inc(s_c, 16)
            for t in range(T):
                sp.dma_start(gb[:, t * D:(t + 1) * D], g_bias.partition_broadcast(P)).then_inc(s_c, 16)
                sp.dma_start(rb[0][:, t * E:(t + 1) * E], br.partition_broadcast(P)).then_inc(s_c, 16)
                sp.dma_start(rb[1][:, t * E:(t + 1) * E], bg.partition_broadcast(P)).then_inc(s_c, 16)
            sp.dma_start(xs[:, :].rearrange("p (n d) -> p n d", d=D), x.rearrange("b (t p) d -> p (b t) d", p=P)).then_inc(s_x, 16)
            sp.dma_start(stage[:, 0:E * H0 // 2].rearrange("p (e h) -> p e h", h=H0), W1a[0:4].rearrange("e d h -> d e h")).then_inc(s_w, 16)
            sp.dma_start(stage[:, E * H0 // 2:E * H0].rearrange("p (e h) -> p e h", h=H0), W1a[4:8].rearrange("e d h -> d e h")).then_inc(s_w, 16)
            sp.dma_start(stage[:, 4096:8192].rearrange("p (e c d) -> p e c d", c=4, d=D), W2a.rearrange("e (c p) d -> p e c d", p=P)).then_inc(s_w, 16)
            sp.wait_ge(s_stage_free, 1)
            sp.dma_start(stage[:, 0:2048].rearrange("p (e h) -> p e h", h=H1), W1b.rearrange("e d h -> d e h")).then_inc(s_w, 16)
            sp.dma_start(stage[:, 2048:4096].rearrange("p (e c d) -> p e c d", c=2, d=D), W2b.rearrange("e (c p) d -> p e c d", p=P)).then_inc(s_w, 16)
            sp.wait_ge(s_stage_free, 2)
            sp.dma_start(stage[:, 4096:4096 + D], W).then_inc(s_w, 16)
            sp.dma_start(stage[:, 4224:4224 + E], Wr).then_inc(s_w, 16)
            sp.dma_start(stage[:, 4240:4240 + E], Wg).then_inc(s_w, 16)

            def load_adj(S, i):
                for j in range(2):
                    sp.wait_ge(S["conv"], 2 * i + j + 1)
                    sp.dma_start(adjI[j][:, :].rearrange("p (t n) -> p t n", n=N),
                                 adj[bass.ds(2 * i + j, 1)].rearrange("o (t p) n -> p (o t) n", p=P)).then_inc(S[f"adj{j}"], 16)

            with sp.Fori(0, NB // 2) as i:
                load_adj(A, i)
            sp.wait_ge(A["conv"], NB + 2)
            with sp.Fori(0, NB // 2) as i:
                load_adj(C, i)
            F = FF[1]
            for b in range(NB):
                sp.wait_ge(F["xadd"], b + 2)
                sp.dma_start(out[b].rearrange("(t p) d -> p t d", p=P),
                             xs[:, b * T * D:(b + 1) * T * D].rearrange("p (t d) -> p t d", d=D)).then_inc(s_x, 16)
            sp.wait_ge(s_x, 16 * (NB + 1))

        @block.gpsimd
        def _(pool):
            nc.gpsimd.memset(epsv[:, :], EPS)
            nc.gpsimd.memset(mhalf[:, :], -0.5).then_inc(s_eps, 1)
            pool.wait_ge(s_eps, 1)
            mark(nc.gpsimd).then_inc(A["conv"], 2)
            mark(nc.gpsimd).then_inc(s_always, 1)
            mark(nc.gpsimd).then_inc(C["conv"], 2)
            pool_rstd(pool, 0, False)
            with pool.Fori(0, NB // 2) as i:
                for j in range(2):
                    wait_alone(pool, (A[f"adj{j}"], 16 * i + 16), (A["agg"], 2 * i + j + 1))
                    nc.gpsimd.tensor_copy(adjF[j][:, :], adjI[j][:, :]).then_inc(A["conv"], 1)
            pool_rstd(pool, 1, True)

            def split_hidden(l, nch):
                F = FF[l]
                with pool.Fori(0, NB * E // 2) as i:
                    for k in range(2):
                        s = 2 * i + k
                        wait_alone(pool, (F["gelu"], nch * (s + 1)), (F["y"], s + 1))
                        nc.gpsimd.tensor_copy(hhi[k][:, 0:nch * N], h32[k][:, 0:nch * N]).then_inc(F["hhi"], 1)

            split_hidden(0, 4)
            pool_rstd(pool, 2, False)
            with pool.Fori(0, NB // 2) as i:
                for j in range(2):
                    wait_alone(pool, (C[f"adj{j}"], 16 * i + 16), (C["bias"], 2 * i + j + 1))
                    nc.gpsimd.tensor_scalar(adjF[j][:, :].bitcast(BF16), adjI[j][:, :], -1.0, -NEG,
                                            ALU.add, ALU.mult).then_inc(C["conv"], 1)
            pool_rstd(pool, 3, False)
            split_hidden(1, 2)

        @block.scalar
        def _(act):
            with act.Fori(0, NB // 2) as i:
                for j in range(2):
                    act.wait_ge(A["tr"], 2 * i + j + 1)
                    act.wait_ge(A["proj"], 2 * i + j + 1)
                    nc.scalar.activation(xTh[j][:, :], bank(j), ACT.Copy).then_inc(A["hi"], 1)
                for j in range(2):
                    act.wait_ge(A["proj"], 2 * i + j + 3)
                    act.wait_ge(A["agg"], 2 * i + j + 1)
                    v = hh[j][:, :].rearrange("p (t d) -> p t d", d=D + 1)
                    nc.scalar.activation(v[:, :, 0:D],
                                         ps[:, 2 + 2 * j:4 + 2 * j, :].rearrange("p k (h d) -> p (k h) d", h=2)[:, :, 0:D],
                                         ACT.Copy).then_inc(A["hh"], 1)

            def gelu_phase(l, nch, hw):
                F = FF[l]

                def steps(b, j, last):
                    for e in range(E):
                        s = 8 * b + e
                        k = e % 2
                        act.wait_ge(F["hlo"], s + 1)
                        for c in range(nch):
                            act.wait_ge(F["up"], nch * s + c + 1)
                            nc.scalar.activation(h32[k][:, c * N:(c + 1) * N], bank(c), ACT.Gelu,
                                                 bias=b1[l][:, e * nch + c:e * nch + c + 1], scale=1.0 / WS
                                                 ).then_inc(F["gelu"], 1)
                        act.wait_ge(F["wb"], s + 1)
                        act.wait_ge(F["comb"], s + 1)
                        nc.scalar.activation(wbs[k][:, :], bank(6), ACT.Copy).then_inc(F["wbc"], 1)
                        if last:
                            continue
                        if e == 2:
                            hi_part(b + 1, 1 - j)
                        if e == 4 and l == 0:
                            tanh_part(b + 1)
                        if e == 6:
                            wt_part(b + 1, 1 - j)

                def hi_part(b, j):
                    act.wait_ge(F["tr"], b + 1)
                    nc.scalar.activation(xTh[j][:, :], bank(7), ACT.Copy).then_inc(F["hi"], 1)

                def tanh_part(b):
                    act.wait_ge(F["d"], b + 1)
                    nc.scalar.activation(ws[:, T:2 * T], ws[:, 0:T], ACT.Tanh, scale=0.5).then_inc(F["th"], 1)

                def wt_part(b, j):
                    act.wait_ge(F["wt"], b + 1)
                    nc.scalar.activation(wT[j][:, :], ps[0:16, 7, 0:N // 2].bitcast(F16), ACT.Copy).then_inc(F["wtc"], 1)

                hi_part(0, 0)
                if l == 0:
                    tanh_part(0)
                wt_part(0, 0)
                with act.Fori(0, NB // 2 - 1) as i:
                    for j in range(2):
                        steps(2 * i + j, j, False)
                steps(NB - 2, 0, False)
                steps(NB - 1, 1, True)

            gelu_phase(0, 4, H0)

            with act.Fori(0, NB // 2) as i:
                for j in range(2):
                    b = 2 * i + j
                    act.wait_ge(C["tr"], b + 1)
                    act.wait_ge(C["proj"], b + 1)
                    nc.scalar.activation(xTh[j][:, :], bank(j), ACT.Copy).then_inc(C["hi"], 1)
                for j in range(2):
                    b = 2 * i + j
                    act.wait_ge(C["proj"], b + 3)
                    act.wait_ge(C["av"], 4 * b + 1)
                    nc.scalar.activation(whE(j)[:, :, 0:D],
                                         ps[:, 2:4, :].rearrange("p k (h d) -> p (k h) d", h=2)[:, :, 0:D],
                                         ACT.Copy).then_inc(C["wh"], 1)
                    act.wait_ge(C["bias"], b + 3)
                    for t in range(T):
                        q = 4 * b + t
                        act.wait_ge(C["p"], q + 1)
                        nc.scalar.activation(eA(t), tt(j, t), ACT.Exp, bias=bi(j, 0, t))
                        nc.scalar.activation(eB(t), tt(j, t), ACT.Exp, bias=bi(j, 1, t), scale=SLOPE).then_inc(C["e"], 1)
                        if t:
                            copy_pt(act, b, t - 1)
                    copy_pt(act, b, T - 1)
                    act.wait_ge(C["mn"], b + 1)
                    nc.scalar.activation(tmpy[:, :], mnb(j), ACT.Exp).then_inc(C["ex"], 1)
            gelu_phase(1, 2, H1)

        @block.tensor
        def _(pe):
            pe.wait_ge(s_ready, 1)
            pe.wait_ge(s_w, 48)
            for e in range(E):
                for c in range(4):
                    last = nc.tensor.matmul(ps[:, 0, e * 4 + c:e * 4 + c + 1], stage[:, e * H0 + c * P:e * H0 + c * P + P],
                                            bT[:, e:e + 1], start=True, stop=True)
            last.then_inc(s_setup_pe, 1)
            pe.wait_ge(s_ready, 2)
            pe.wait_ge(s_w, 16 * 8)
            nc.tensor.transpose(ps[:, 1, 0:P], stage[:, 4096:4096 + D], idf[:, :])
            nc.tensor.matmul(ps[:, 2, 0:2], stage[:, 4096:4096 + D], acol[:, :], start=True, stop=True).then_inc(s_setup_pe, 1)

            pe.wait_ge(s_ready, 3)
            with pe.Fori(0, NB // 2) as i:
                for j in range(2):
                    b = 2 * i + j
                    pe.wait_ge(A["xn"], b + 1)
                    pe.wait_ge(A["lo"], b + 1)
                    transpose_tiles(pe, bank(j), xn[j]).then_inc(A["tr"], 1)
                for j in range(2):
                    b = 2 * i + j
                    pe.wait_ge(A["lo"], b + 3)
                    pe.wait_ge(A["upd"], b + 1)
                    for t in range(T):
                        o = ps[:, 2 + 2 * j + t // 2, (t % 2) * 256:(t % 2) * 256 + 256]
                        xh, xl = xTh[j][:, t * P:(t + 1) * P], xTl[j][:, t * P:(t + 1) * P]
                        nc.tensor.matmul(o, xh, wA[0][:, :], start=True, stop=False)
                        nc.tensor.matmul(o, xh, wA[1][:, :], start=False, stop=False)
                        last = nc.tensor.matmul(o, xl, wA[0][:, :], start=False, stop=True)
                    last.then_inc(A["proj"], 1)
                for j in range(2):
                    b = 2 * i + j
                    pe.wait_ge(A["upd"], b + 3)
                    pe.wait_ge(A["conv"], b + 3)
                    pe.wait_ge(A["read"], b + 1)
                    for q in range(T):
                        o = ps[:, 6 + q // 2, (q % 2) * 256:(q % 2) * 256 + D + 1]
                        for t in range(T):
                            lhs = adjF[j][:, t * N + q * P:t * N + q * P + P]
                            nc.tensor.matmul(o, lhs, hh[j][:, t * (D + 1):(t + 1) * (D + 1)],
                                             start=(t == 0), stop=False)
                            last = nc.tensor.matmul(o[:, 0:D], lhs, hl[j][:, t * D:(t + 1) * D],
                                                    start=False, stop=(t == T - 1))
                    last.then_inc(A["agg"], 1)

            def expert_phase(l, nch):
                F = FF[l]
                hw = nch * P

                def up(b, j, e):
                    s = 8 * b + e
                    if e == 0:
                        pe.wait_ge(F["lo"], b + 1)
                    for c in range(nch):
                        if isinstance(s, int) and s == 0:
                            pass
                        else:
                            pe.wait_ge(F["gelu"], nch * (s - 1) + c + 1)
                        o = bank(c)
                        wh = w1[l][0][:, e * hw + c * P:e * hw + c * P + P]
                        wl = w1[l][1][:, e * hw + c * P:e * hw + c * P + P]
                        nc.tensor.matmul(o, wh, xTh[j][:, :], start=True, stop=False)
                        nc.tensor.matmul(o, wh, xTl[j][:, :], start=False, stop=False)
                        nc.tensor.matmul(o, wl, xTh[j][:, :], start=False, stop=True).then_inc(F["up"], 1)

                def weights_row(b, j, e):
                    s = 8 * b + e
                    if e == 0:
                        pe.wait_ge(F["wtc"], b + 1)
                    pe.wait_ge(F["wbc"], s + 1)
                    nc.tensor.matmul(bank(6), selh[:, e * P:(e + 1) * P], wT[j][:, :], start=True, stop=True).then_inc(F["wb"], 1)

                def down(b, e):
                    s = 8 * b + e
                    k = e % 2
                    pe.wait_ge(F["hlo"], s + 3)
                    pe.wait_ge(F["comb"], s + 1)
                    o = bank(4 + k)
                    for c in range(nch):
                        wh = w2[l][0][:, (e * nch + c) * D:(e * nch + c + 1) * D]
                        wl = w2[l][1][:, (e * nch + c) * D:(e * nch + c + 1) * D]
                        nc.tensor.matmul(o, wh, hhi[k][:, c * N:(c + 1) * N], start=(c == 0), stop=False)
                        nc.tensor.matmul(o, wh, hlo[k][:, c * N:(c + 1) * N], start=False, stop=False)
                        last = nc.tensor.matmul(o, wl, hhi[k][:, c * N:(c + 1) * N], start=False, stop=(c == nch - 1))
                    last.then_inc(F["y"], 1)

                def tr_part(b, j):
                    pe.wait_ge(F["xn"], b + 1)
                    if not (isinstance(b, int) and b == 0):
                        pe.wait_ge(F["xadd"], b)
                    transpose_tiles(pe, bank(7), xn[j]).then_inc(F["tr"], 1)

                def lg_part(b, j):
                    pe.wait_ge(F["lo"], b + 1)
                    for t in range(T):
                        o = ps[:, 7, t * E:(t + 1) * E]
                        xh, xl = xTh[j][:, t * P:(t + 1) * P], xTl[j][:, t * P:(t + 1) * P]
                        nc.tensor.matmul(o, xh, wR[l][0][:, :], start=True, stop=False)
                        nc.tensor.matmul(o, xh, wR[l][1][:, :], start=False, stop=False)
                        last = nc.tensor.matmul(o, xl, wR[l][0][:, :], start=False, stop=True)
                    last.then_inc(F["lg"], 1)

                def wt_part(b, j):
                    pe.wait_ge(F["rt"], b + 1)
                    v = ps[0:16, 7, 0:N // 2].bitcast(F16)
                    for t in range(T):
                        last = nc.tensor.transpose(v[:, t * P:(t + 1) * P], w16[:, t * 16:(t + 1) * 16], idh[:, :])
                    last.then_inc(F["wt"], 1)

                def final(b, j):
                    pe.wait_ge(F["comb"], 8 * b + 10)
                    if not (isinstance(b, int) and b == 15):
                        pe.wait_ge(F["wtc"], b + 2)
                    for t in range(T):
                        o = ps[:, 7, t * D:(t + 1) * D]
                        w = wT[j][:, t * P:(t + 1) * P]
                        nc.tensor.matmul(o, acc[j][:, t * P:(t + 1) * P], idf[:, :], start=True, stop=False)
                        nc.tensor.matmul(o, w, b2[l][0][:, :], start=False, stop=False)
                        last = nc.tensor.matmul(o, w, b2[l][1][:, :], start=False, stop=True)
                    last.then_inc(F["fin"], 1)

                def batch(b, j, last):
                    for e in range(E):
                        if e < E - 1:
                            up(b, j, e + 1)
                        elif not last:
                            up(b + 1, 1 - j, 0)
                        weights_row(b, j, e)
                        down(b, e)
                        if not last:
                            if e == 1:
                                tr_part(b + 1, 1 - j)
                            if e == 3:
                                lg_part(b + 1, 1 - j)
                            if e == 5:
                                wt_part(b + 1, 1 - j)
                    final(b, j)

                tr_part(0, 0)
                lg_part(0, 0)
                wt_part(0, 0)
                up(0, 0, 0)
                with pe.Fori(0, NB // 2 - 1) as i:
                    for j in range(2):
                        batch(2 * i + j, j, False)
                batch(NB - 2, 0, False)
                batch(NB - 1, 1, True)

            expert_phase(0, 4)

            with pe.Fori(0, NB // 2) as i:
                for j in range(2):
                    b = 2 * i + j
                    pe.wait_ge(C["xn"], b + 1)
                    pe.wait_ge(C["lo"], b + 1)
                    transpose_tiles(pe, bank(j), xn[j]).then_inc(C["tr"], 1)
                for j in range(2):
                    b = 2 * i + j
                    pe.wait_ge(C["lo"], b + 3)
                    pe.wait_ge(C["bias"], b + 2)
                    for t in range(T):
                        o = ps[:, 2 + t // 2, (t % 2) * 256:(t % 2) * 256 + D + 2]
                        xh, xl = xTh[j][:, t * P:(t + 1) * P], xTl[j][:, t * P:(t + 1) * P]
                        nc.tensor.matmul(o, xh, wC[0][:, :], start=True, stop=False)
                        nc.tensor.matmul(o, xh, wC[1][:, :], start=False, stop=False)
                        nc.tensor.matmul(o, xl, wC[0][:, :], start=False, stop=True)
                    nc.tensor.matmul(bank(7), wS[0][:, :], xTh[j][:, :], start=True, stop=False)
                    nc.tensor.matmul(bank(7), wS[0][:, :], xTl[j][:, :], start=False, stop=False)
                    nc.tensor.matmul(bank(7), wS[1][:, :], xTh[j][:, :], start=False, stop=True).then_inc(C["proj"], 1)

                    def p_transposes(t):
                        q = 4 * b + t
                        pe.wait_ge(C["p"], q + 3)
                        pe.wait_ge(C["pt"], q + 1)
                        for c in range(T):
                            last = nc.tensor.transpose(ps[:, 4 + t % 2, c * P:(c + 1) * P],
                                                       pm(t)[:, c * P:(c + 1) * P], idf[:, :])
                        last.then_inc(C["ptr"], 1)

                    def p_times_wh(t):
                        q = 4 * b + t
                        pe.wait_ge(C["pt"], q + 3)
                        pe.wait_ge(C["wh"], b + 1)
                        pe.wait_ge(C["fin"], q + 1)
                        for c in range(T):
                            last = nc.tensor.matmul(ps[:, 6, 0:D + 1], PT(t)[:, c * P:(c + 1) * P], whE(j)[:, c, :],
                                                    start=(c == 0), stop=(c == T - 1))
                        last.then_inc(C["av"], 1)

                    p_transposes(0)
                    for t in range(1, T):
                        p_transposes(t)
                        p_times_wh(t - 1)
                    p_times_wh(T - 1)

            expert_phase(1, 2)

        @block.vector
        def _(dve):
            ch = Chain(dve, s_ch)
            for j in range(2):
                nc.vector.memset(hh[j][:, :].rearrange("p (t d) -> p t d", d=D + 1)[:, :, D:D + 1], 1.0)
                nc.vector.memset(acc_w[j][:, :].rearrange("p (t d) -> p t d", d=D + 1)[:, :, D:D + 1], 1.0)
            credits = [(A, "lo", 2), (A, "proj", 2), (A, "upd", 2), (A, "agg", 2), (A, "read", 1), (C, "lo", 2),
                       (C, "proj", 2), (C, "bias", 2), (C, "av", 8), (C, "p", 2), (C, "pt", 2), (C, "fin", 1)]
            for F in FF:
                credits += [(F, "hlo", 2), (F, "y", 2), (F, "comb", 2), (F, "wbc", 1), (F, "xadd", 1)]
            for S, name, k in credits:
                mark(nc.vector).then_inc(S[name], k)

            dve.wait_ge(s_c, 16 * 27)

            def split(hi, lo, src):
                ch(nc.vector.tensor_copy(hi, src))
                nc.vector.tensor_tensor(lo, src, hi, ALU.subtract)

            split(wA[0][:, :], wA[1][:, :], smf[:, 0:2 * D])
            for l in range(2):
                ch(nc.vector.tensor_scalar(b2f[:, l * D:(l + 1) * D], b2f[:, l * D:(l + 1) * D], WS, None, ALU.mult))
                split(b2[l][0][:, :], b2[l][1][:, :], b2f[:, l * D:(l + 1) * D])
            ch(mark(nc.vector))
            mark(nc.vector).then_inc(s_ready, 1)
            dve.wait_ge(s_setup_pe, 1)
            ch(nc.vector.tensor_tensor(b1[0][:, :], b1[0][:, :], ps[:, 0, 0:32], ALU.add))
            for e in range(E):
                ch(nc.vector.tensor_scalar(stage[:, e * H0:(e + 1) * H0], stage[:, e * H0:(e + 1) * H0], gT[:, e:e + 1], WS,
                                           ALU.mult, ALU.mult))
            ch(nc.vector.tensor_copy(w1[0][0][:, :], stage[:, 0:4096]))
            nc.vector.tensor_tensor(w1[0][1][:, :], stage[:, 0:4096], w1[0][0][:, :], ALU.subtract).then_inc(s_stage_free, 1)
            ch(nc.vector.tensor_scalar(stage[:, 4096:8192], stage[:, 4096:8192], WS, None, ALU.mult))
            ch(nc.vector.tensor_copy(w2[0][0][:, :], stage[:, 4096:8192]))
            nc.vector.tensor_tensor(w2[0][1][:, :], stage[:, 4096:8192], w2[0][0][:, :], ALU.subtract).then_inc(s_stage_free, 1)
            dve.wait_ge(s_w, 16 * 8)
            ch(nc.vector.tensor_scalar(stage[:, 0:4096], stage[:, 0:4096], WS, None, ALU.mult))
            split(w1[1][0][:, :], w1[1][1][:, :], stage[:, 0:2048])
            split(w2[1][0][:, :], w2[1][1][:, :], stage[:, 2048:4096])
            split(wR[0][0][:, :], wR[0][1][:, :], stage[:, 4224:4224 + E])
            split(wR[1][0][:, :], wR[1][1][:, :], stage[:, 4240:4240 + E])
            mark(nc.vector).then_inc(s_ready, 1)
            dve.wait_ge(s_setup_pe, 2)
            ch(nc.vector.tensor_copy(smf[:, 0:D], ps[:, 1, 0:P]))
            ch(nc.vector.tensor_copy(smf[:, D:D + 2], ps[:, 2, 0:2]))
            split(wC[0][:, :], wC[1][:, :], smf[:, 0:D + 2])
            ch(mark(nc.vector))
            for k in range(2):
                ch(nc.vector.tensor_copy(wS[k][:, :], wC[k][:, D + 1:D + 2].to_broadcast([P, P])))
            mark(nc.vector).then_inc(s_ready, 1)

            dve.wait_ge(s_x, 16)
            for b in range(NB):
                for t in range(T):
                    ch(nc.vector.bn_stats(st6[:, 6 * t:6 * t + 6], xs[:, (b * T + t) * D:(b * T + t + 1) * D]))
                for t in range(T):
                    last = nc.vector.bn_aggr(mv[:, 2 * (b * T + t):2 * (b * T + t) + 2], st6[:, 6 * t:6 * t + 6])
                ch(last)
            mark(nc.vector).then_inc(s_st[0], 1)
            dve.wait_ge(s_rs[0], 1)

            cA = Chain(dve, A["ch"])
            SA = 10
            with dve.Fori(0, NB // 2) as i:
                cA.start(SA * i)
                for j in range(2):
                    b = 2 * i + j
                    normalise(dve, b, j).then_inc(A["xn"], 1)
                for j in range(2):
                    b = 2 * i + j
                    dve.wait_ge(A["hi"], b + 1)
                    dve.wait_ge(A["proj"], b + 1)
                    nc.vector.tensor_tensor(xTl[j][:, :], bank(j), xTh[j][:, :], ALU.subtract).then_inc(A["lo"], 1)
                for j in range(2):
                    b = 2 * i + j
                    dve.wait_ge(A["hh"], b + 1)
                    dve.wait_ge(A["agg"], b + 1)
                    pv = ps[:, 2 + 2 * j:4 + 2 * j, :].rearrange("p k (h d) -> p (k h) d", h=2)
                    nc.vector.tensor_tensor(v3(hl[j][:, :], D), pv[:, :, 0:D],
                                            hh[j][:, :].rearrange("p (t d) -> p t d", d=D + 1)[:, :, 0:D],
                                            ALU.subtract)
                    nc.vector.tensor_tensor(v3(upd[j][:, :], D), pv[:, :, D:2 * D], v3(gb[:, :], D),
                                            ALU.add).then_inc(A["upd"], 1)
                for j in range(2):
                    b = 2 * i + j
                    dve.wait_ge(A["agg"], b + 3)
                    dve.wait_ge(A["upd"], b + 3)
                    av = ps[:, 6:8, :].rearrange("p k (h d) -> p (k h) d", h=2)
                    cA(nc.vector.tensor_scalar(deg[j][:, 0:T].rearrange("p (t o) -> p t o", o=1), av[:, :, D:D + 1],
                                               1.0, None, ALU.max))
                    cA(nc.vector.reciprocal(deg[j][:, T:2 * T], deg[j][:, 0:T]))
                    for t in range(T):
                        ins = nc.vector.scalar_tensor_tensor(upd[j][:, t * D:(t + 1) * D], av[:, t, 0:D],
                                                             deg[j][:, T + t:T + t + 1], upd[j][:, t * D:(t + 1) * D],
                                                             ALU.mult, ALU.add)
                    ins.then_inc(A["read"], 1)
                    dve.wait_ge(A["read"], b + 2)
                    xb = xs[:, bass.ds(b * (T * D), T * D)]
                    cA(nc.vector.scalar_tensor_tensor(xb, upd[j][:, :], 0.0, xb, ALU.max, ALU.add), wait_alone)
                    for t in range(T):
                        last = nc.vector.bn_stats(st6[:, 6 * t:6 * t + 6], xs[:, bass.ds(b * (T * D) + t * D, D)])
                    cA(last, wait_alone)
                    aggregate(cA, b, mv).then_inc(s_st[1], 1)
                    dve.wait_ge(s_st[1], b + 1)
                assert cA.k == SA, cA.k

            def expert_phase(l, nch):
                F = FF[l]
                ce = Chain(dve, F["ch"])
                SE = (23, 16)[l]

                def lo_part(b, j):
                    dve.wait_ge(F["hi"], b + 1)
                    nc.vector.tensor_tensor(xTl[j][:, :], bank(7), xTh[j][:, :], ALU.subtract).then_inc(F["lo"], 1)

                def route1(b, j):
                    dve.wait_ge(F["lg"], b + 1)
                    if l == 0:
                        ce(nc.vector.tensor_tensor(v3(lg[:, :], E), v3(ps[:, 7, 0:T * E], E),
                                                   cinv[:, bass.ds(b * T, T)].rearrange("p (t o) -> p t o", o=1).to_broadcast([P, T, E]),
                                                   ALU.mult))
                        ce(nc.vector.tensor_tensor(lg[:, :], lg[:, :], rb[0][:, :], ALU.add), wait_alone)
                    else:
                        ce(nc.vector.tensor_tensor(lg[:, :], ps[:, 7, 0:T * E], rb[1][:, :], ALU.add), wait_alone)
                    for t in range(T):
                        last = nc.vector.max(mx8[:, t * E:(t + 1) * E], lg[:, t * E:(t + 1) * E])
                    ce(last, wait_alone)
                    for t in range(T):
                        last = nc.vector.max_index(ix8[:, t * E:(t + 1) * E], mx8[:, t * E:(t + 1) * E], lg[:, t * E:(t + 1) * E])
                    ce(last)
                    ce(nc.vector.tensor_copy(ixf[:, :], ix8[:, :]))
                    if l == 0:
                        nc.vector.tensor_tensor(ws[:, 0:T].rearrange("p (t o) -> p t o", o=1), v3(mx8[:, :], E)[:, :, 0:1],
                                                v3(mx8[:, :], E)[:, :, 1:2], ALU.subtract).then_inc(F["d"], 1)

                def route2(b, j):
                    for k in range(2):
                        ce(nc.vector.tensor_tensor(v3(oh[:, k * T * E:(k + 1) * T * E], E), v3(io8[:, :], E),
                                                   v3(ixf[:, :], E)[:, :, k:k + 1].to_broadcast([P, T, E]), ALU.is_equal))
                    if l == 0:
                        dve.wait_ge(F["th"], b + 1)
                        ce(nc.vector.tensor_scalar(ws[:, 2 * T:3 * T], ws[:, T:2 * T], 0.5 / WS, 0.5 / WS, ALU.mult, ALU.add))
                        ce(nc.vector.tensor_scalar(ws[:, 3 * T:4 * T], ws[:, T:2 * T], -0.5 / WS, 0.5 / WS, ALU.mult, ALU.add))
                        for k in range(2):
                            o = v3(oh[:, k * T * E:(k + 1) * T * E], E)
                            ce(nc.vector.tensor_tensor(o, o, ws[:, (2 + k) * T:(3 + k) * T].rearrange("p (t o) -> p t o", o=1).to_broadcast([P, T, E]), ALU.mult))
                        ce(nc.vector.tensor_tensor(oh[:, 0:T * E], oh[:, 0:T * E], oh[:, T * E:2 * T * E], ALU.add))
                    else:
                        ce(nc.vector.tensor_tensor(oh[:, 0:T * E], oh[:, 0:T * E], oh[:, T * E:2 * T * E], ALU.add))
                        ce(nc.vector.tensor_scalar(oh[:, 0:T * E], oh[:, 0:T * E], 1.0 / WS, None, ALU.mult))
                    wv = v3(w16[:, :], 16)
                    ce(nc.vector.tensor_copy(wv[:, :, 0:E], v3(oh[:, 0:T * E], E)))
                    nc.vector.tensor_tensor(wv[:, :, E:2 * E], v3(oh[:, 0:T * E], E), wv[:, :, 0:E], ALU.subtract).then_inc(F["rt"], 1)

                def hid_lo(b, e):
                    s = 8 * b + e
                    k = e % 2
                    dve.wait_ge(F["hhi"], s + 1)
                    dve.wait_ge(F["y"], s + 1)
                    nc.vector.tensor_tensor(hlo[k][:, 0:nch * N], h32[k][:, 0:nch * N], hhi[k][:, 0:nch * N],
                                            ALU.subtract).then_inc(F["hlo"], 1)

                def combine(b, j, e):
                    s = 8 * b + e
                    k = e % 2
                    dve.wait_ge(F["y"], s + 3)
                    dve.wait_ge(F["wbc"], s + 2)
                    if e == 0:
                        nc.vector.tensor_tensor(acc[j][:, :], bank(4 + k), wbs[k][:, :], ALU.mult).then_inc(F["comb"], 1)
                    else:
                        dve.wait_ge(F["comb"], s + 2)
                        ce(nc.vector.tensor_tensor(tmpy[:, :], bank(4 + k), wbs[k][:, :], ALU.mult))
                        nc.vector.tensor_tensor(acc[j][:, :], acc[j][:, :], tmpy[:, :], ALU.add).then_inc(F["comb"], 1)

                def add_to_x(b, j):
                    dve.wait_ge(F["fin"], b + 1)
                    xb = xs[:, bass.ds(b * (T * D), T * D)]
                    nc.vector.tensor_tensor(xb, xb, bank(7), ALU.add).then_inc(F["xadd"], 1)
                    if l == 0:
                        wait_alone(dve, (F["xadd"], b + 2))
                        for t in range(T):
                            last = nc.vector.bn_stats(st6[:, 6 * t:6 * t + 6], xs[:, bass.ds(b * (T * D) + t * D, D)])
                        ce(last, wait_alone)
                        ce(aggregate(ce, b, mv3))

                def batch(b, j, last):
                    ce.start(SE * b + S0)
                    for e in range(E):
                        hid_lo(b, e)
                        if e:
                            combine(b, j, e - 1)
                        if not last:
                            if e == 1:
                                normalise(dve, b + 1, 1 - j).then_inc(F["xn"], 1)
                            if e == 3:
                                lo_part(b + 1, 1 - j)
                            if e == 4:
                                route1(b + 1, 1 - j)
                            if e == 5:
                                route2(b + 1, 1 - j)
                    combine(b, j, E - 1)
                    add_to_x(b, j)
                    assert last or ce.k == SE, ("E", l, ce.k)

                dve.wait_ge(s_rs[1 + 2 * l], 1)
                ce.start(0)
                normalise(dve, 0, 0).then_inc(F["xn"], 1)
                lo_part(0, 0)
                route1(0, 0)
                route2(0, 0)
                S0 = ce.k
                with dve.Fori(0, NB // 2 - 1) as i:
                    for j in range(2):
                        batch(2 * i + j, j, False)
                batch(NB - 2, 0, False)
                batch(NB - 1, 1, True)
            expert_phase(0, 4)
            ch(nc.vector.tensor_copy(mv[:, :], mv3[:, :]))
            mark(nc.vector).then_inc(s_st[2], NB)
            dve.wait_ge(s_rs[2], 1)

            cC = Chain(dve, C["ch"])
            SC = 24
            with dve.Fori(0, NB // 2) as i:
                cC.start(SC * i)
                for j in range(2):
                    normalise(dve, 2 * i + j, j).then_inc(C["xn"], 1)
                for j in range(2):
                    b = 2 * i + j
                    dve.wait_ge(C["hi"], b + 1)
                    dve.wait_ge(C["proj"], b + 1)
                    nc.vector.tensor_tensor(xTl[j][:, :], bank(j), xTh[j][:, :], ALU.subtract).then_inc(C["lo"], 1)
                for j in range(2):
                    b = 2 * i + j
                    wait_alone(dve, (C["proj"], b + 3), (C["conv"], b + 3))
                    R = rowb[:, j * 8 * T:(j + 1) * 8 * T]
                    M = R[:, 2 * T:3 * T]
                    for t in range(T):
                        last = nc.vector.tensor_tensor_reduce(
                            out=tt(j, t), in0=bank(7), in1=adjF[j][:, t * N:(t + 1) * N].bitcast(BF16), scale=1.0,
                            scalar=-3.0e38, op0=ALU.add, op1=ALU.max, accum_out=M[:, t:t + 1])
                    cC(last)
                    s1 = R[:, 3 * T:4 * T]
                    sv = ps[:, 2:4, :].rearrange("p k (h d) -> p (k h) d", h=2)
                    dve.wait_ge(C["wh"], b + 1)
                    cC(nc.vector.tensor_copy(s1.rearrange("p (t o) -> p t o", o=1), sv[:, :, D:D + 1]))
                    cC(nc.vector.tensor_tensor(M, M, s1, ALU.add))
                    cC(nc.vector.scalar_tensor_tensor(R[:, 4 * T:5 * T], M, SLOPE, M, ALU.mult, ALU.max))
                    nc.vector.tensor_tensor(R[:, 0:T], s1, R[:, 4 * T:5 * T], ALU.subtract)
                    nc.vector.scalar_tensor_tensor(R[:, T:2 * T], s1, SLOPE, R[:, 4 * T:5 * T], ALU.mult,
                                                   ALU.subtract).then_inc(C["bias"], 1)

                    def take_max(t):
                        q = 4 * b + t
                        dve.wait_ge(C["e"], q + 1)
                        nc.vector.tensor_tensor(pm(t), eA(t), eB(t), ALU.max).then_inc(C["p"], 1)

                    def evict(t):
                        q = 4 * b + t
                        dve.wait_ge(C["av"], q + 9)
                        cC(nc.vector.reciprocal(R[:, 5 * T + t:5 * T + t + 1], ps[:, 6, D:D + 1]))
                        nc.vector.tensor_scalar(hpb(j)[:, t * D:(t + 1) * D], ps[:, 6, 0:D], R[:, 5 * T + t:5 * T + t + 1],
                                                None, ALU.mult).then_inc(C["fin"], 1)

                    for t in range(T):
                        if t >= 2:
                            dve.wait_ge(C["ptr"], 4 * b + t - 1)
                        take_max(t)
                        if t >= 2:
                            evict(t - 2)
                    evict(T - 2)
                    evict(T - 1)
                    dve.wait_ge(C["fin"], 4 * b + 5)
                    nc.vector.tensor_scalar(mnb(j), hpb(j), 0.0, None, ALU.min).then_inc(C["mn"], 1)
                    xb = xs[:, bass.ds(b * (T * D), T * D)]
                    cC(nc.vector.scalar_tensor_tensor(xb, hpb(j), 0.0, xb, ALU.max, ALU.add))
                    dve.wait_ge(C["ex"], b + 1)
                    cC(nc.vector.scalar_tensor_tensor(xb, tmpy[:, :], -1.0, xb, ALU.add, ALU.add), wait_alone)
                    for t in range(T):
                        last = nc.vector.bn_stats(st6[:, 6 * t:6 * t + 6], xs[:, bass.ds(b * (T * D) + t * D, D)])
                    cC(last, wait_alone)
                    aggregate(cC, b, mv).then_inc(s_st[3], 1)
                    dve.wait_ge(s_st[3], b + 1)
                assert cC.k == SC, ("C", cC.k)

            expert_phase(1, 2)


_INS = ['x', 'adj', 'L0_gnn_W_msg', 'L0_gnn_W_upd', 'L0_gnn_bias', 'L0_ffn_Wr', 'L0_ffn_br', 'L0_ffn_ln_g', 'L0_ffn_ln_b',
        'L0_ffn_W1', 'L0_ffn_b1', 'L0_ffn_W2', 'L0_ffn_b2', 'L1_gnn_W', 'L1_gnn_a', 'L1_ffn_Wg', 'L1_ffn_bg', 'L1_ffn_W1',
        'L1_ffn_b1', 'L1_ffn_W2', 'L1_ffn_b2']


def kernel(**inputs):
    import concourse.bacc as _bacc
    from concourse.bass_utils import run_bass_kernel_spmd as _run

    nc = _bacc.Bacc("TRN2", target_bir_lowering=False, num_devices=1)
    arrays, args = {}, []

    def give(name, a):
        arrays[name] = a
        args.append(nc.dram_tensor(name, a.shape, mybir.dt.from_np(a.dtype), kind="ExternalInput").ap())

    for name in _INS:
        give(f"in_{name}_dram", np.ascontiguousarray(inputs[name]))
    give("c_identf", np.eye(P, dtype=np.float32))
    give("c_identh", np.eye(P, dtype=np.float16))
    sel = np.zeros((16, E, P), np.float16)
    for e in range(E):
        sel[e, e] = sel[e + E, e] = 1
    give("c_sel", sel.reshape(16, E * P))
    give("c_iota8", np.tile(np.arange(E, dtype=np.float32), (P, T)))
    args.append(nc.dram_tensor("out_0_dram", (NB, N, D), F32, kind="ExternalOutput").ap())
    build(nc, *args)
    r = _run(nc, [arrays], core_ids=[0])
    return r.results[0]["out_0_dram"]
```

```python
import numpy as np
import concourse.bass as bass
from concourse import mybir
from contextlib import ExitStack

P = 128
NB, N, D = 16, 512, 128
T = N // P
NT = NB * T
NP = NB // 2
TP = 2 * T
TOK = NB * N
E, K = 8, 2
HID = (512, 256)
G = 256
NQ = TOK * K // G + E
CAP = TOK + G
ROW = 288
NOWHERE = 1 << 20
EPS = 1e-5
SLOPE = 0.2
NEG = -float(2 ** 53)
WS = 64.0

F32, F16, BF16 = mybir.dt.float32, mybir.dt.float16, mybir.dt.bfloat16
I32, U32 = mybir.dt.int32, mybir.dt.uint32
ALU = mybir.AluOpType
ACT = mybir.ActivationFunctionType
AX = mybir.AxisListType


class Chain:

    def __init__(self, eng, sem):
        self.eng, self.sem, self.base, self.k = eng, sem, 0, 0

    def __call__(self, ins, alone=None):
        self.k += 1
        ins.then_inc(self.sem, 1)
        if alone:
            alone(self.eng, (self.sem, self.base + self.k))
        else:
            self.eng.wait_ge(self.sem, self.base + self.k)

    def enter(self, i, first, steps):
        self.before, self.steps = self.base + self.k, steps
        self.base, self.k = (i - first) * steps + self.before, 0

    def leave(self, rounds):
        assert self.k == self.steps, f"CHAIN {self.k} for {self.steps}"
        self.base, self.k = self.before + rounds * self.steps, 0


def build(nc, x, adj, W_msg, W_upd, g_bias, Wr, br, ln_g, ln_b, W1a, b1a, W2a, b2a,
          W, a, Wg, bg, W1b, b1b, W2b, b2b, identf, identh, lower, iota8, ids, iotaq, out):
    ctx = ExitStack()
    with ctx:
        def sb(name, shape, dt=F32):
            return ctx.enter_context(nc.sbuf_tensor(name, shape, dt))

        def sem(name):
            return ctx.enter_context(nc.semaphore(name))

        def sems(prefix, names):
            return {n: sem(f"{prefix}_{n}") for n in names.split()}

        slots = [nc.dram_tensor(f"slots{l}", [E * CAP + G, ROW], F16).ap() for l in range(2)]
        ys = [nc.dram_tensor(f"ys{l}", [K * TOK, D], F32).ap() for l in range(2)]

        xs = sb("xs", [P, NT * D])
        mv = sb("mv", [P, NT * 2])
        rs = sb("rs", [P, NT])
        ps = ctx.enter_context(nc.psum_tensor("ps", [P, 8, 512], F32))
        idf = sb("idf", [P, P])
        idh = sb("idh", [P, P], F16)
        low = sb("low", [P, 2 * P], F16)
        io8 = sb("io8", [P, TP * E])
        ebase = sb("ebase", [P, TP * E])
        idt = sb("idt", [P, NP * K * TP], U32)
        ioq = sb("ioq", [1, NQ * E])
        mhalf = sb("mhalf", [P, NT])
        zt = sb("zt", [P, 64])
        cells = iter(range(64))

        stage = sb("stage", [P, 8192])
        wA = [sb(f"wA{k}", [P, 2 * D], F16) for k in range(2)]
        wC = [sb(f"wC{k}", [P, D + 2], F16) for k in range(2)]
        wS = [sb(f"wS{k}", [P, P], F16) for k in range(2)]
        wR = [[sb(f"wR{l}{k}", [P, E], F16) for k in range(2)] for l in range(2)]
        wx = [sb(f"wx{l}", [P, E * 4 * HID[l]], F16) for l in range(2)]
        NC = [h // P for h in HID]
        bx = [sb(f"bx{l}", [P, E * (NC[l] + 1)]) for l in range(2)]
        gb = sb("gb", [P, D])
        rb = [sb(f"rb{l}", [P, E]) for l in range(2)]
        gT = sb("gT", [P, E])
        bT = sb("bT", [P, E])
        acol = sb("acol", [P, 2])

        adjI = [sb(f"adjI{j}", [P, T * N], I32) for j in range(2)]
        adjF = [sb(f"adjF{j}", [P, T * N], F16) for j in range(2)]
        xn = [sb(f"xn{j}", [P, T * D]) for j in range(2)]
        xTh = [sb(f"xTh{j}", [P, N], F16) for j in range(2)]
        xTl = [sb(f"xTl{j}", [P, N], F16) for j in range(2)]
        hh = [sb(f"hh{j}", [P, T * (D + 1)], F16) for j in range(2)]
        hl = [sb(f"hl{j}", [P, T * D], F16) for j in range(2)]
        upd = [sb(f"upd{j}", [P, T * D]) for j in range(2)]
        deg = [sb(f"deg{j}", [P, 2 * T]) for j in range(2)]
        whE = [sb(f"whE{j}", [P, T * (D + 1)]) for j in range(2)]
        rowb = [sb(f"rowb{j}", [P, 6 * T]) for j in range(2)]
        st6 = sb("st6", [P, TP * 6])
        mvc = sb("mvc", [P, TP * 2])
        uc = sb("uc", [P, TP])
        rc = sb("rc", [P, TP])
        mvr = sb("mvr", [P, TP * 2])
        ur = sb("ur", [P, 2 * TP])
        rr = sb("rr", [P, 2 * TP])
        cinv = sb("cinv", [P, TP])
        xr = sb("xr", [P, TP * D])
        smf, wcf, Wf = xr[:, 0:2 * D + 16], xr[:, 3 * D:4 * D + 2], xr[:, 5 * D:6 * D]
        rows = sb("rows", [P, K * TP * ROW], F16)
        xTr = sb("xTr", [P, TP * 2 * P], F16)
        lg = sb("lg", [P, TP * E])
        mx8 = sb("mx8", [P, TP * E])
        ix8 = sb("ix8", [P, TP * E], U32)
        ixf = sb("ixf", [P, TP * E])
        oh = [sb(f"oh{k}", [P, TP * E]) for k in range(K)]
        mk = sb("mk", [P, TP * E], F16)
        run = [sb(f"run{l}", [P, E], F16) for l in range(2)]
        cnt = sb("cnt", [P, E])
        dd = sb("dd", [P, 2 * TP])
        pos = sb("pos", [P, TP * E])
        tm8 = sb("tm8", [P, TP * E])
        posf = sb("posf", [P, K * TP])
        posi = sb("posi", [P, K * TP], U32)
        wts = sb("wts", [P, NT * K])
        padr = sb("padr", [P, 2 * ROW], F16)
        tf = sb("tf", [1, 8 * E])
        ti = sb("ti", [1, E], I32)
        tq = sb("tq", [1, 2 * NQ * E])
        tr = sb("tr", [1, 4 * NQ])
        tab = [sb(f"tab{l}", [1, 2 * NQ + E], I32) for l in range(2)]
        gx = [rows[:, k * 2 * ROW:(k + 1) * 2 * ROW] for k in range(4)]
        xg = [xTr[:, k * 2 * G:(k + 1) * 2 * G] for k in range(2)]
        yT = [xTr[:, (4 + 2 * k) * G:(6 + 2 * k) * G].bitcast(F32) for k in range(2)]
        idc = [sb(f"idc{k}", [P, 2], U32) for k in range(4)]
        bcur = [sb(f"bcur{k}", [P, NC[0] + 1]) for k in range(2)]
        h32 = [sb(f"h32{k}", [P, 4 * G]) for k in range(2)]
        hhi = [adjF[k][:, 0:4 * G] for k in range(2)]
        hlo = [adjF[k][:, 4 * G:8 * G] for k in range(2)]
        yrows = sb("yrows", [P, 4 * G])
        yrow = [yrows[:, k * G:(k + 1) * G] for k in range(4)]
        yb = h32
        hpb = upd
        mnb = [yrows[:, j * T * D:(j + 1) * T * D] for j in range(2)]

        s_c = sem("s_c")
        s_x = [sem(f"s_x{q}") for q in range(4)]
        s_w = [sem(f"s_w{l}") for l in range(2)]
        s_p = sem("s_p")
        s_q = sem("s_q")
        s_ch = sem("s_ch")
        s_m = sem("s_m")
        s_st = sem("s_st")
        s_rs = sem("s_rs")
        s_always = sem("s_always")
        s_out = sem("s_out")
        s_cb = sem("s_cb")
        A = sems("A", "adj0 adj1 conv xn tr hi lo proj hh upd agg read fin")
        C = sems("C", "adj0 adj1 y0 y1 conv comb u r xn tr hi lo proj wh bias e p ptr pt av fin mn ex")
        R = [sems(f"R{l}", "u r xr hi rows t x lg mk d th pf pos sc cnt tab pad") for l in range(2)]
        M = [sems(f"M{l}", "ld0 ld1 ld2 ld3 t xg up bc gelu lo y yt ytt yr sc0 sc1 sc2 sc3") for l in range(2)]
        Z = sems("Z", "y0 y1 add")

        block = ctx.enter_context(nc.Block())

        def bank(k):
            return ps[:, k, :]

        def v3(ap, k):
            return ap.rearrange("p (t k) -> p t k", k=k)

        def col(ap):
            return ap.rearrange("p (t o) -> p t o", o=1)

        def rows_of(k, lo, hi):
            return rows[:, k * TP * ROW:(k + 1) * TP * ROW].rearrange("p (t r) -> p t r", r=ROW)[:, :, lo:hi]

        def wait(eng, semaphore, value):
            if not isinstance(value, int) or value > 0:
                eng.wait_ge(semaphore, value)

        def wait_alone(eng, *pairs):
            pairs = [(s, v if isinstance(v, int) else eng.to_reg(v)) for s, v in pairs if not isinstance(v, int) or v > 0]
            eng.wait_ge(s_always, 1)
            for s, v in pairs:
                eng.wait_ge(s, v)

        def mark(eng):
            c = next(cells)
            return eng.memset(zt[:, c:c + 1], 0.0)

        def xpair(i):
            return xs[:, bass.ds(i * (TP * D), TP * D)]

        def xbatch(b):
            return xs[:, bass.ds(b * (T * D), T * D)]

        def xtile(n):
            return xs[:, bass.ds(n * D, D)]

        def tt(j, t):
            return stage[:, (j * T + t) * N:(j * T + t + 1) * N]

        def part(k, t):
            return stage[:, 4096 + (2 * k + t % 2) * N:4096 + (2 * k + t % 2 + 1) * N]

        def pairs_of(eng, body, chain=None, steps=0):
            body(0, None)
            body(1, 0)
            with eng.Fori(2, NP) as i:
                if chain:
                    chain.enter(i, 2, steps)
                body(i, i - 1)
            if chain:
                chain.leave(NP - 2)
            body(None, NP - 1)

        def groups(eng, body, chain=None, steps=0):
            for n in range(6):
                body(n, n % 4)
            with eng.Fori(1, NQ // 4 - 1) as i:
                if chain:
                    chain.enter(i, 1, steps)
                for d in range(4):
                    body(4 * i + 2 + d, (2 + d) % 4)
            if chain:
                chain.leave(NQ // 4 - 2)
            body(NQ - 2, 2)

        def rounds(n, k4):
            return n // 4 if isinstance(n, int) else (n - k4) // 4

        @block.sync
        def _(sp):
            def slow(dst, src, s):
                sp.dma_start(dst, src, allow_slow_non_contiguous=True).then_inc(s, 16)

            for q in range(4):
                n = NT // 4
                sp.dma_start(xs[:, q * n * D:(q + 1) * n * D].rearrange("p (n d) -> p n d", d=D),
                             x[q * NB // 4:(q + 1) * NB // 4].rearrange("b (t p) d -> p (b t) d", p=P)).then_inc(s_x[q], 16)
            sp.dma_start(smf[:, 0:D], W_msg).then_inc(s_c, 16)
            sp.dma_start(smf[:, D:2 * D], W_upd).then_inc(s_c, 16)
            sp.dma_start(smf[:, 2 * D:2 * D + 8], Wr).then_inc(s_c, 16)
            sp.dma_start(smf[:, 2 * D + 8:2 * D + 16], Wg).then_inc(s_c, 16)
            sp.dma_start(idf[:, :], identf).then_inc(s_c, 16)
            sp.dma_start(idh[:, :], identh).then_inc(s_c, 16)
            sp.dma_start(low[:, :], lower).then_inc(s_c, 16)
            sp.dma_start(io8[:, :], iota8[0]).then_inc(s_c, 16)
            sp.dma_start(ebase[:, :], iota8[1]).then_inc(s_c, 16)
            sp.dma_start(idt[:, :], ids).then_inc(s_c, 16)
            sp.dma_start(ioq[:, :], iotaq).then_inc(s_c, 16)
            sp.dma_start(Wf[:, :], W).then_inc(s_c, 16)
            sp.dma_start(gb[:, :], g_bias.partition_broadcast(P)).then_inc(s_c, 16)
            sp.dma_start(rb[0][:, :], br.partition_broadcast(P)).then_inc(s_c, 16)
            sp.dma_start(rb[1][:, :], bg.partition_broadcast(P)).then_inc(s_c, 16)
            slow(acol[:, :], a.rearrange("(k o) one -> o (k one)", k=2), s_c)

            def load_adj(S, i):
                for j in range(2):
                    wait(sp, S["conv"], 2 * i + j - 1)
                    sp.dma_start(adjI[j][:, :].rearrange("p (t n) -> p t n", n=N),
                                 adj[bass.ds(2 * i + j, 1)].rearrange("o (t p) n -> p (o t) n", p=P)
                                 ).then_inc(S[f"adj{j}"], 16)

            load_adj(A, 0)
            for h in range(2):
                sp.dma_start(stage[:, 2048 * h:2048 * (h + 1)].rearrange("p (e h) -> p e h", h=HID[0]),
                             W1a[4 * h:4 * h + 4].rearrange("e d h -> d e h")).then_inc(s_w[0], 16)
                sp.dma_start(stage[:, 4096 + 2048 * h:4096 + 2048 * (h + 1)].rearrange("p (e c d) -> p e c d", c=4, d=D),
                             W2a[4 * h:4 * h + 4].rearrange("e (c p) d -> p e c d", p=P)).then_inc(s_w[0], 16)
            slow(gT[:, :], ln_g.rearrange("e d -> d e"), s_w[0])
            slow(bT[:, :], ln_b.rearrange("e d -> d e"), s_w[0])
            for l, b1, b2 in ((0, b1a, b2a), (1, b1b, b2b)):
                v = bx[l][:, :].rearrange("p (e c) -> p e c", c=NC[l] + 1)
                for c in range(NC[l]):
                    slow(v[:, :, c:c + 1], b1[:, c * P:(c + 1) * P].rearrange("e (p o) -> p e o", o=1), s_w[0])
                slow(v[:, :, NC[l]:NC[l] + 1], b2.rearrange("e (p o) -> p e o", o=1), s_w[0])
            load_adj(A, 1)
            with sp.Fori(2, NP) as i:
                load_adj(A, i)

            def pads(l):
                sp.wait_ge(R[l]["tab"], 1)
                sp.wait_ge(s_m, 3)
                for e in range(E + 1):
                    at = E * CAP
                    if e < E:
                        at = sp.value_load(tab[l][0:1, 2 * NQ + e:2 * NQ + e + 1], min_val=0, max_val=E * CAP)
                    sp.dma_start(slots[l][bass.ds(at, G), :].rearrange("(p h) r -> p (h r)", h=2), padr[:, :]
                                 ).then_inc(R[l]["pad"], 16)

            def fetch(l, n, k):
                S = M[l]
                wait(sp, S["t"], n - 3)
                wait(sp, S["xg"], n - 3)
                at = sp.value_load(tab[l][0:1, bass.ds(n, 1)], min_val=0, max_val=E * CAP)
                sp.dma_start(gx[k][:, :], slots[l][bass.ds(at, G), :].rearrange("(p h) r -> p (h r)", h=2)
                             ).then_inc(S[f"ld{k}"], 16)

            def fetch_all(l):
                sp.wait_ge(R[l]["sc"], 16 * K * NT)
                sp.wait_ge(R[l]["pad"], 16 * (E + 1))
                for n in range(4):
                    fetch(l, n, n)
                with sp.Fori(1, NQ // 4) as i:
                    for k in range(4):
                        fetch(l, 4 * i + k, k)

            def scattered(l):
                for k in range(4):
                    sp.wait_ge(M[l][f"sc{k}"], 32 * (NQ // 4))

            def load_y(l, S, b, j, used):
                wait(sp, S[used], b - 1)
                for k in range(K):
                    sp.dma_start(yb[j][:, k * N:(k + 1) * N].rearrange("p (t d) -> p t d", d=D),
                                 ys[l].rearrange("(n p) d -> p n d", p=P)[:, bass.ds(b * T + k * NT, T), :]
                                 ).then_inc(S[f"y{j}"], 16)

            pads(0)
            fetch_all(0)
            sp.wait_ge(s_q, 3)
            sp.dma_start(stage[:, 0:2048].rearrange("p (e h) -> p e h", h=HID[1]), W1b.rearrange("e d h -> d e h")).then_inc(s_w[1], 16)
            sp.dma_start(stage[:, 4096:6144].rearrange("p (e c d) -> p e c d", c=2, d=D),
                         W2b.rearrange("e (c p) d -> p e c d", p=P)).then_inc(s_w[1], 16)
            sp.wait_ge(A["conv"], NB)
            load_adj(C, 0)
            scattered(0)

            def graph1(i):
                for j in range(2):
                    load_y(0, C, 2 * i + j, j, "comb")

            graph1(0)
            load_adj(C, 1)
            graph1(1)
            with sp.Fori(2, NP) as i:
                graph1(i)
                load_adj(C, i)
            pads(1)
            fetch_all(1)
            scattered(1)

            def last(i):
                for j in range(2):
                    load_y(1, Z, 2 * i + j, j, "add")

            def store(b):
                sp.wait_ge(Z["add"], b + 1)
                sp.dma_start(out[bass.ds(b, 1)].rearrange("o (t p) d -> p (o t) d", p=P),
                             xbatch(b).rearrange("p (t d) -> p t d", d=D)).then_inc(s_out, 16)

            last(0)
            with sp.Fori(1, NP) as i:
                last(i)
                for j in range(2):
                    store(2 * i + j - 2)
            store(NB - 2)
            store(NB - 1)
            sp.wait_ge(s_out, 16 * NB)

        @block.gpsimd
        def _(pool):
            mark(nc.gpsimd).then_inc(s_always, 1)
            nc.gpsimd.memset(mhalf[:, :], -0.5).then_inc(s_m, 1)
            pool.wait_ge(s_st, 1)
            pool.wait_ge(s_m, 3)
            nc.gpsimd.tensor_tensor(rs[:, :], rs[:, :], mhalf[:, :], ALU.pow).then_inc(s_rs, 1)

            def masks(S, i, used, add, mult, dt):
                for j in range(2):
                    b = 2 * i + j
                    wait_alone(pool, (S[f"adj{j}"], 16 * i + 16), (S[used], b - 1))
                    nc.gpsimd.tensor_scalar(adjF[j][:, :].bitcast(dt), adjI[j][:, :], add, mult, ALU.add, ALU.mult
                                            ).then_inc(S["conv"], 1)

            def route_power(l, p):
                pool.wait_ge(R[l]["u"], p + 1)
                n = 2 * TP if l == 0 else TP
                nc.gpsimd.tensor_tensor(rr[:, 0:n], ur[:, 0:n], mhalf[:, 0:n], ALU.pow).then_inc(R[l]["r"], 1)

            def scatter(l, p):
                wait_alone(pool, (R[l]["rows"], p + 1), (R[l]["pos"], p + 1))
                for k in range(K):
                    for t in range(TP):
                        nc.gpsimd.indirect_dma_start(
                            slots[l], bass.IndirectOffsetOnAxis(ap=posi[:, k * TP + t:k * TP + t + 1], axis=0),
                            rows[:, (k * TP + t) * ROW:(k * TP + t + 1) * ROW], None).then_inc(R[l]["sc"], 16)

            def body_a(i, p):
                if p is not None:
                    route_power(0, p)
                if i is not None:
                    masks(A, i, "agg", 0.0, 1.0, F16)
                if p is not None:
                    scatter(0, p)

            def body_c(i, p):
                if i is not None:
                    pool.wait_ge(C["u"], i + 1)
                    nc.gpsimd.tensor_tensor(rc[:, :], uc[:, :], mhalf[:, 0:TP], ALU.pow).then_inc(C["r"], 1)
                if p is not None:
                    route_power(1, p)
                if i is not None:
                    masks(C, i, "bias", -1.0, -NEG, BF16)
                if p is not None:
                    scatter(1, p)

            def put_back(l, n, k):
                S = M[l]
                wait_alone(pool, (S["yr"], n + 1))
                for h in range(2):
                    nc.gpsimd.indirect_dma_start(
                        ys[l], bass.IndirectOffsetOnAxis(ap=idc[k][:, h:h + 1], axis=0), yrow[k][:, h * D:(h + 1) * D], None,
                        bounds_check=K * TOK - 1, oob_is_err=False).then_inc(S[f"sc{k}"], 16)

            pairs_of(pool, body_a)
            with pool.Fori(0, NQ // 4) as i:
                for k in range(4):
                    put_back(0, 4 * i + k, k)
            pairs_of(pool, body_c)
            with pool.Fori(0, NQ // 4) as i:
                for k in range(4):
                    put_back(1, 4 * i + k, k)

        @block.scalar
        def _(act):
            def graph_hi(S, i):
                for j in range(2):
                    b = 2 * i + j
                    wait(act, S["proj"], b - 1)
                    act.wait_ge(S["tr"], b + 1)
                    nc.scalar.activation(xTh[j][:, :], bank(0), ACT.Copy).then_inc(S["hi"], 1)

            def route_hi(l, p):
                wait(act, R[l]["sc"], 16 * K * TP * p)
                act.wait_ge(R[l]["xr"], p + 1)
                nc.scalar.activation(rows_of(0, 0, D), v3(xr[:, :], D), ACT.Copy).then_inc(R[l]["hi"], 1)

            def route_x(l, p):
                for j in range(2):
                    act.wait_ge(R[l]["t"], 2 * p + j + 1)
                    nc.scalar.activation(xTr[:, j * 8 * P:(j + 1) * 8 * P], bank(0).bitcast(F16), ACT.Copy
                                         ).then_inc(R[l]["x"], 1)

            def route_tanh(p):
                act.wait_ge(R[0]["d"], p + 1)
                nc.scalar.activation(dd[:, TP:2 * TP], dd[:, 0:TP], ACT.Tanh, scale=0.5).then_inc(R[0]["th"], 1)

            def halves(lo, hi):
                return ps[:, lo:lo + 2, :].rearrange("p k (h d) -> p (k h) d", h=2)[:, :, 0:hi]

            def hh_part(b, j):
                wait(act, A["agg"], b - 1)
                act.wait_ge(A["proj"], b + 1)
                nc.scalar.activation(v3(hh[j][:, :], D + 1)[:, :, 0:D], halves(2, D), ACT.Copy).then_inc(A["hh"], 1)

            def body_a(i, p):
                if i is not None:
                    graph_hi(A, i)
                if p is not None:
                    route_hi(0, p)
                if i is not None:
                    hh_part(2 * i, 0)
                if p is not None:
                    route_x(0, p)
                if i is not None:
                    hh_part(2 * i + 1, 1)
                if p is not None:
                    route_tanh(p)

            pairs_of(act, body_a)

            def experts(l):
                S, nc_ = M[l], NC[l]

                def hidden(n, k, k4):
                    wait(act, S["yt"], n - 1)
                    e = act.value_load(tab[l][0:1, bass.ds(n + NQ, 1)], min_val=0, max_val=E - 1)
                    nc.scalar.activation(bcur[k][:, 0:nc_ + 1], bx[l][:, bass.ds(e * (nc_ + 1), nc_ + 1)], ACT.Copy
                                         ).then_inc(S["bc"], 1)
                    act.wait_ge(S["bc"], n + 1)
                    wait(act, S["lo"], n - 1)
                    for c in range(nc_):
                        if c % 2 == 0:
                            act.wait_ge(S["up"], nc_ // 2 * n + c // 2 + 1)
                        nc.scalar.activation(h32[k][:, c * G:(c + 1) * G],
                                             ps[:, 2 * k + c // 2, (c % 2) * G:(c % 2 + 1) * G], ACT.Gelu,
                                             bias=bcur[k][:, c:c + 1], scale=1.0 / WS).then_inc(S["gelu"], 1)

                def result(n, k, k4):
                    act.wait_ge(S["y"], n + 1)
                    wait(act, S["ytt"], n - 1)
                    nc.scalar.activation(yT[k][:, :], ps[:, 4 + k, 0:G], ACT.Identity,
                                         bias=bcur[k][:, nc_:nc_ + 1], scale=1.0 / WS).then_inc(S["yt"], 1)

                act.wait_ge(R[l]["tab"], 1)
                act.wait_ge(s_q, (3, 4)[l])
                hidden(0, 0, 0)

                def body(n, k4):
                    hidden(n + 1, (k4 + 1) % 2, (k4 + 1) % 4)
                    result(n, k4 % 2, k4)

                groups(act, body)
                result(NQ - 1, 1, 3)

            experts(0)

            def wh_part(b, j):
                wait(act, C["av"], 4 * b - 4)
                act.wait_ge(C["proj"], b + 1)
                nc.scalar.activation(v3(whE[j][:, :], D + 1)[:, :, 0:D], halves(2, D), ACT.Copy).then_inc(C["wh"], 1)

            def copy_pt(b, t):
                q = 4 * b + t
                act.wait_ge(C["ptr"], q + 1)
                wait(act, C["av"], q - 1)
                nc.scalar.activation(part(3, t), bank(4 + t % 2), ACT.Copy).then_inc(C["pt"], 1)

            def exps(b, j):
                act.wait_ge(C["bias"], b + 1)
                for t in range(T):
                    wait(act, C["p"], 4 * b + t - 1)
                    nc.scalar.activation(part(0, t), tt(j, t), ACT.Exp, bias=rowb[j][:, t:t + 1])
                    nc.scalar.activation(part(1, t), tt(j, t), ACT.Exp, bias=rowb[j][:, T + t:T + t + 1],
                                         scale=SLOPE).then_inc(C["e"], 1)
                    if t:
                        copy_pt(b, t - 1)
                copy_pt(b, T - 1)
                act.wait_ge(C["mn"], b + 1)
                nc.scalar.activation(mnb[j][:, :], mnb[j][:, :], ACT.Exp).then_inc(C["ex"], 1)

            def body_c(i, p):
                if i is not None:
                    graph_hi(C, i)
                if p is not None:
                    route_hi(1, p)
                if i is not None:
                    wh_part(2 * i, 0)
                if p is not None:
                    route_x(1, p)
                if i is not None:
                    exps(2 * i, 0)
                    wh_part(2 * i + 1, 1)
                    exps(2 * i + 1, 1)

            pairs_of(act, body_c)
            experts(1)

        @block.tensor
        def _(pe):
            pe.wait_ge(s_c, 16 * 16)
            nc.tensor.transpose(ps[:, 6, 0:P], Wf[:, :], idf[:, :])
            nc.tensor.matmul(ps[:, 7, 0:2], Wf[:, :], acol[:, :], start=True, stop=True).then_inc(s_p, 1)

            def graph_t(S, i, evacuated):
                for j in range(2):
                    b = 2 * i + j
                    pe.wait_ge(S["xn"], b + 1)
                    wait(pe, S["lo"], b)
                    if j == 0:
                        wait(pe, evacuated, 2 * i - 2)
                    for t in range(T):
                        last = nc.tensor.transpose(ps[:, 0, t * P:(t + 1) * P], xn[j][:, t * D:(t + 1) * D], idf[:, :])
                    last.then_inc(S["tr"], 1)

            def route_t(l, p, S):
                pe.wait_ge(R[l]["rows"], p + 1)
                pe.wait_ge(S["lo"], min(2 * p + 4, NB) if isinstance(p, int) else 2 * p + 4)
                for j in range(2):
                    wait(pe, R[l]["x"], 2 * p + j)
                    v = bank(0).bitcast(F16)
                    for t in range(T):
                        for part_ in range(2):
                            o = (t * 2 + part_) * P
                            src = (j * T + t) * ROW + part_ * D
                            last = nc.tensor.transpose(v[:, o:o + P], rows[:, src:src + D], idh[:, :])
                    last.then_inc(R[l]["t"], 1)

            def route_scores(l, p):
                pe.wait_ge(R[l]["x"], 2 * p + 2)
                wait(pe, R[l]["pos"], p)
                for t in range(TP):
                    o = ps[:, 1, t * E:(t + 1) * E]
                    xh, xl = xTr[:, 2 * t * P:(2 * t + 1) * P], xTr[:, (2 * t + 1) * P:(2 * t + 2) * P]
                    nc.tensor.matmul(o, xh, wR[l][0][:, :], start=True, stop=False)
                    nc.tensor.matmul(o, xh, wR[l][1][:, :], start=False, stop=False)
                    last = nc.tensor.matmul(o, xl, wR[l][0][:, :], start=False, stop=True)
                last.then_inc(R[l]["lg"], 1)

            def route_prefix(l, p):
                pe.wait_ge(R[l]["mk"], p + 1)
                for t in range(TP):
                    o = ps[:, 1, (TP + t) * E:(TP + t + 1) * E]
                    nc.tensor.matmul(o, low[:, P:2 * P], run[l][:, :], start=True, stop=False)
                    for s in range(t):
                        nc.tensor.matmul(o, low[:, P:2 * P], mk[:, s * E:(s + 1) * E], start=False, stop=False)
                    last = nc.tensor.matmul(o, low[:, 0:P], mk[:, t * E:(t + 1) * E], start=False, stop=True)
                last.then_inc(R[l]["pf"], 1)

            def count(l):
                pe.wait_ge(R[l]["pos"], NP)
                pe.wait_ge(R[l]["cnt"], NP)
                nc.tensor.matmul(ps[:, 1, 0:E], low[:, P:2 * P], run[l][:, :], start=True, stop=True).then_inc(R[l]["pf"], 1)

            def project_a(b, j):
                pe.wait_ge(A["lo"], b + 1)
                wait(pe, A["upd"], b)
                for t in range(T):
                    o = ps[:, 2 + t // 2, (t % 2) * 256:(t % 2) * 256 + 256]
                    xh, xl = xTh[j][:, t * P:(t + 1) * P], xTl[j][:, t * P:(t + 1) * P]
                    nc.tensor.matmul(o, xh, wA[0][:, :], start=True, stop=False)
                    nc.tensor.matmul(o, xh, wA[1][:, :], start=False, stop=False)
                    last = nc.tensor.matmul(o, xl, wA[0][:, :], start=False, stop=True)
                last.then_inc(A["proj"], 1)

            def aggregate(b, j):
                pe.wait_ge(A["upd"], b + 1)
                pe.wait_ge(A["conv"], b + 1)
                wait(pe, A["read"], b)
                for q in range(T):
                    o = ps[:, 4 + q // 2, (q % 2) * 256:(q % 2) * 256 + D + 1]
                    for t in range(T):
                        lhs = adjF[j][:, t * N + q * P:t * N + q * P + P]
                        nc.tensor.matmul(o, lhs, hh[j][:, t * (D + 1):(t + 1) * (D + 1)], start=(t == 0), stop=False)
                        last = nc.tensor.matmul(o[:, 0:D], lhs, hl[j][:, t * D:(t + 1) * D], start=False, stop=(t == T - 1))
                last.then_inc(A["agg"], 1)

            def body_a(i, p):
                if i is not None:
                    graph_t(A, i, R[0]["x"])
                    project_a(2 * i, 0)
                if p is not None:
                    route_t(0, p, A)
                    route_scores(0, p)
                if i is not None:
                    project_a(2 * i + 1, 1)
                    aggregate(2 * i, 0)
                if p is not None:
                    route_prefix(0, p)
                if i is not None:
                    aggregate(2 * i + 1, 1)

            pe.wait_ge(s_q, 1)
            pairs_of(pe, body_a)
            pe.wait_ge(s_w[0], 16 * 14)
            for e in range(E):
                for c in range(4):
                    last = nc.tensor.matmul(ps[:, 2, e * 4 + c:e * 4 + c + 1], stage[:, e * 512 + c * P:e * 512 + c * P + P],
                                            bT[:, e:e + 1], start=True, stop=True)
            last.then_inc(s_p, 1)
            count(0)

            def experts(l):
                S, nc_, hw = M[l], NC[l], HID[l]

                def turn(n, k4):
                    pe.wait_ge(S[f"ld{k4}"], rounds(n, k4) * 16 + 16)
                    wait(pe, S["xg"], n)
                    v = bank(6).bitcast(F16)
                    for part_ in range(2):
                        for h in range(2):
                            o = (part_ * 2 + h) * P
                            last = nc.tensor.transpose(v[:, o:o + P], gx[k4][:, h * ROW + part_ * D:h * ROW + part_ * D + D],
                                                       idh[:, :])
                    last.then_inc(S["t"], 1)

                def up(n, k):
                    e = pe.value_load(tab[l][0:1, bass.ds(n + NQ, 1)], min_val=0, max_val=E - 1)
                    pe.wait_ge(S["xg"], n + 1)
                    wait(pe, S["gelu"], nc_ * (n - 1))
                    for c in range(nc_):
                        o = ps[:, 2 * k + c // 2, (c % 2) * G:(c % 2 + 1) * G]
                        wh = wx[l][:, bass.ds(e * (4 * hw) + c * P, P)]
                        wl = wx[l][:, bass.ds(e * (4 * hw) + hw + c * P, P)]
                        nc.tensor.matmul(o, wh, xg[k][:, 0:G], start=True, stop=False)
                        nc.tensor.matmul(o, wh, xg[k][:, G:2 * G], start=False, stop=False)
                        last = nc.tensor.matmul(o, wl, xg[k][:, 0:G], start=False, stop=True)
                        if c % 2:
                            last.then_inc(S["up"], 1)

                def down(n, k):
                    e = pe.value_load(tab[l][0:1, bass.ds(n + NQ, 1)], min_val=0, max_val=E - 1)
                    pe.wait_ge(S["lo"], n + 1)
                    wait(pe, S["yt"], n - 1)
                    o = ps[:, 4 + k, 0:G]
                    for c in range(nc_):
                        wh = wx[l][:, bass.ds(e * (4 * hw) + 2 * hw + c * P, P)]
                        wl = wx[l][:, bass.ds(e * (4 * hw) + 3 * hw + c * P, P)]
                        nc.tensor.matmul(o, wh, hhi[k][:, c * G:(c + 1) * G], start=(c == 0), stop=False)
                        nc.tensor.matmul(o, wh, hlo[k][:, c * G:(c + 1) * G], start=False, stop=False)
                        last = nc.tensor.matmul(o, wl, hhi[k][:, c * G:(c + 1) * G], start=False, stop=(c == nc_ - 1))
                    last.then_inc(S["y"], 1)

                def turn_back(n, k):
                    pe.wait_ge(S["yt"], n + 1)
                    wait(pe, S["yr"], n)
                    for h in range(2):
                        last = nc.tensor.transpose(ps[:, 7, h * P:(h + 1) * P], yT[k][:, h * P:(h + 1) * P], idf[:, :])
                    last.then_inc(S["ytt"], 1)

                pe.wait_ge(R[l]["tab"], 1)
                pe.wait_ge(s_q, (3, 4)[l])
                turn(0, 0)
                turn(1, 1)
                up(0, 0)

                def body(n, k4):
                    k = k4 % 2
                    up(n + 1, 1 - k)
                    if not (isinstance(n, int) and n + 2 >= NQ):
                        turn(n + 2, (k4 + 2) % 4)
                    if not (isinstance(n, int) and n == 0):
                        turn_back(n - 1, 1 - k)
                    down(n, k)

                groups(pe, body)
                turn_back(NQ - 2, 0)
                down(NQ - 1, 1)
                turn_back(NQ - 1, 1)

            experts(0)

            def project_c(b, j):
                pe.wait_ge(C["lo"], b + 1)
                wait(pe, C["bias"], b)
                for t in range(T):
                    o = ps[:, 2 + t // 2, (t % 2) * 256:(t % 2) * 256 + D + 2]
                    xh, xl = xTh[j][:, t * P:(t + 1) * P], xTl[j][:, t * P:(t + 1) * P]
                    nc.tensor.matmul(o, xh, wC[0][:, :], start=True, stop=False)
                    nc.tensor.matmul(o, xh, wC[1][:, :], start=False, stop=False)
                    nc.tensor.matmul(o, xl, wC[0][:, :], start=False, stop=True)
                nc.tensor.matmul(bank(7), wS[0][:, :], xTh[j][:, :], start=True, stop=False)
                nc.tensor.matmul(bank(7), wS[0][:, :], xTl[j][:, :], start=False, stop=False)
                nc.tensor.matmul(bank(7), wS[1][:, :], xTh[j][:, :], start=False, stop=True).then_inc(C["proj"], 1)

            def attend(b, j):
                def turn_p(t):
                    q = 4 * b + t
                    pe.wait_ge(C["p"], q + 1)
                    wait(pe, C["pt"], q - 1)
                    for c in range(T):
                        last = nc.tensor.transpose(ps[:, 4 + t % 2, c * P:(c + 1) * P], part(2, t)[:, c * P:(c + 1) * P],
                                                   idf[:, :])
                    last.then_inc(C["ptr"], 1)

                def times(t):
                    q = 4 * b + t
                    pe.wait_ge(C["pt"], q + 1)
                    pe.wait_ge(C["wh"], b + 1)
                    wait(pe, C["fin"], q)
                    for c in range(T):
                        last = nc.tensor.matmul(ps[:, 6, 0:D + 1], part(3, t)[:, c * P:(c + 1) * P],
                                                whE[j][:, c * (D + 1):(c + 1) * (D + 1)], start=(c == 0), stop=(c == T - 1))
                    last.then_inc(C["av"], 1)

                turn_p(0)
                for t in range(1, T):
                    turn_p(t)
                    times(t - 1)
                times(T - 1)

            def body_c(i, p):
                if i is not None:
                    graph_t(C, i, R[1]["x"])
                    project_c(2 * i, 0)
                if p is not None:
                    route_t(1, p, C)
                    route_scores(1, p)
                    route_prefix(1, p)
                if i is not None:
                    attend(2 * i, 0)
                    project_c(2 * i + 1, 1)
                    attend(2 * i + 1, 1)

            pairs_of(pe, body_c)
            count(1)
            experts(1)

        @block.vector
        def _(dve):
            ch = Chain(dve, s_ch)
            nc.vector.memset(zt[:, 63:64], 0.0)
            for j in range(2):
                nc.vector.memset(v3(hh[j][:, :], D + 1)[:, :, D:D + 1], 1.0)
                nc.vector.memset(v3(whE[j][:, :], D + 1)[:, :, D:D + 1], 1.0)
                nc.vector.memset(run[j][:, :], 0.0)
            nc.vector.memset(rows[:, :].bitcast(U32), 0)
            ch(nc.vector.memset(padr[:, :].bitcast(U32), 0))
            nc.vector.memset(padr[:, :].bitcast(U32).rearrange("p (h r) -> p h r", h=2)[:, :, D:D + 1], NOWHERE).then_inc(s_m, 1)

            def split(hi, lo, src):
                ch(nc.vector.tensor_copy(hi, src))
                nc.vector.tensor_tensor(lo, src, hi, ALU.subtract)

            for q in range(4):
                dve.wait_ge(s_x[q], 16)
                for half in range(2):
                    n0 = q * (NT // 4) + half * TP
                    for t in range(TP):
                        last = nc.vector.bn_stats(st6[:, 6 * t:6 * t + 6], xs[:, (n0 + t) * D:(n0 + t + 1) * D])
                    ch(last)
                    for t in range(TP):
                        last = nc.vector.bn_aggr(mv[:, 2 * (n0 + t):2 * (n0 + t) + 2], st6[:, 6 * t:6 * t + 6])
                    ch(last)
            nc.vector.tensor_scalar(rs[:, :], v3(mv[:, :], 2)[:, :, 1], EPS, None, ALU.add).then_inc(s_st, 1)
            mark(nc.vector).then_inc(s_m, 1)
            dve.wait_ge(s_c, 16 * 16)
            split(wA[0][:, :], wA[1][:, :], smf[:, 0:2 * D])
            for l in range(2):
                split(wR[l][0][:, :], wR[l][1][:, :], smf[:, 2 * D + 8 * l:2 * D + 8 * l + 8])
            dve.wait_ge(s_p, 1)
            ch(nc.vector.tensor_copy(wcf[:, 0:D], ps[:, 6, 0:P]))
            ch(nc.vector.tensor_copy(wcf[:, D:D + 2], ps[:, 7, 0:2]))
            split(wC[0][:, :], wC[1][:, :], wcf[:, :])
            ch(mark(nc.vector))
            for k in range(2):
                last = nc.vector.tensor_copy(wS[k][:, :], wC[k][:, D + 1:D + 2].to_broadcast([P, P]))
            ch(last)
            mark(nc.vector).then_inc(s_q, 1)
            dve.wait_ge(s_rs, 1)

            def statistics(mvx, n0, static=False):
                for t in range(TP):
                    last = nc.vector.bn_stats(st6[:, 6 * t:6 * t + 6], xtile(n0 + t))
                ch(last, wait_alone)
                for t in range(TP):
                    last = nc.vector.bn_aggr(mvx[:, 2 * t:2 * t + 2], st6[:, 6 * t:6 * t + 6])
                ch(last)

            def lo_part(S, i):
                for j in range(2):
                    b = 2 * i + j
                    dve.wait_ge(S["hi"], b + 1)
                    wait(dve, S["proj"], b - 1)
                    nc.vector.tensor_tensor(xTl[j][:, :], bank(0), xTh[j][:, :], ALU.subtract).then_inc(S["lo"], 1)

            def route_stats(l, p):
                statistics(mvr, p * TP)
                v = col(mvr[:, :].rearrange("p (t two) -> p two t", two=2)[:, 1, :])
                if l == 0:
                    nc.vector.tensor_scalar(col(ur[:, 0:TP]), v, 1.0 + EPS, EPS * EPS, ALU.mult, ALU.add)
                    nc.vector.tensor_scalar(col(ur[:, TP:2 * TP]), v, EPS, None, ALU.add).then_inc(R[l]["u"], 1)
                else:
                    nc.vector.tensor_scalar(col(ur[:, 0:TP]), v, EPS, None, ALU.add).then_inc(R[l]["u"], 1)

            def route_norm(l, p):
                dve.wait_ge(R[l]["r"], p + 1)
                if l == 0:
                    ch(nc.vector.tensor_tensor(cinv[:, :], ur[:, 0:TP], rr[:, 0:TP], ALU.mult))
                    ch(nc.vector.tensor_tensor(cinv[:, :], cinv[:, :], rr[:, TP:2 * TP], ALU.mult))
                for t in range(TP):
                    last = nc.vector.tensor_scalar(xr[:, t * D:(t + 1) * D], xtile(p * TP + t), mvr[:, 2 * t:2 * t + 1],
                                                   rr[:, t:t + 1], ALU.subtract, ALU.mult)
                last.then_inc(R[l]["xr"], 1)

            def route_rows(l, p):
                dve.wait_ge(R[l]["hi"], p + 1)
                nc.vector.tensor_tensor(rows_of(0, D, 2 * D), v3(xr[:, :], D), rows_of(0, 0, D), ALU.subtract)
                ch(nc.vector.tensor_copy(rows[:, :].bitcast(U32).rearrange("p (n r) -> p n r", r=ROW // 2)[:, :, D:D + 1],
                                         col(idt[:, bass.ds(p * (K * TP), K * TP)])))
                nc.vector.tensor_copy(rows_of(1, 0, 2 * D), rows_of(0, 0, 2 * D)).then_inc(R[l]["rows"], 1)

            def bcast(ap, n):
                return ap.to_broadcast([P, n, E])

            def route_choose(l, p):
                dve.wait_ge(R[l]["lg"], p + 1)
                sc = v3(ps[:, 1, 0:TP * E], E)
                rbv = rb[l][:, :].rearrange("p (o e) -> p o e", o=1).to_broadcast([P, TP, E])
                if l == 0:
                    ch(nc.vector.tensor_tensor(v3(lg[:, :], E), sc, bcast(col(cinv[:, :]), TP), ALU.mult))
                    ch(nc.vector.tensor_tensor(v3(lg[:, :], E), v3(lg[:, :], E), rbv, ALU.add), wait_alone)
                else:
                    ch(nc.vector.tensor_tensor(v3(lg[:, :], E), sc, rbv, ALU.add), wait_alone)
                for t in range(TP):
                    last = nc.vector.max(mx8[:, t * E:(t + 1) * E], lg[:, t * E:(t + 1) * E])
                ch(last, wait_alone)
                for t in range(TP):
                    last = nc.vector.max_index(ix8[:, t * E:(t + 1) * E], mx8[:, t * E:(t + 1) * E], lg[:, t * E:(t + 1) * E])
                ch(last)
                if l == 0:
                    nc.vector.tensor_tensor(col(dd[:, 0:TP]), v3(mx8[:, :], E)[:, :, 0:1], v3(mx8[:, :], E)[:, :, 1:2],
                                            ALU.subtract).then_inc(R[0]["d"], 1)
                ch(nc.vector.tensor_copy(ixf[:, :], ix8[:, :]))
                for k in range(K):
                    last = nc.vector.tensor_tensor(v3(oh[k][:, :], E), v3(io8[:, :], E),
                                                   bcast(v3(ixf[:, :], E)[:, :, k:k + 1], TP), ALU.is_equal)
                ch(last)
                nc.vector.tensor_tensor(mk[:, :], oh[0][:, :], oh[1][:, :], ALU.add).then_inc(R[l]["mk"], 1)

            def route_places(l, p):
                if l == 0:
                    dve.wait_ge(R[0]["th"], p + 1)
                    w = wts[:, bass.ds(p * (TP * K), TP * K)].rearrange("p (t k) -> p t k", k=K)
                    nc.vector.tensor_scalar(w[:, :, 0:1], col(dd[:, TP:2 * TP]), 0.5, 0.5, ALU.mult, ALU.add)
                    nc.vector.tensor_scalar(w[:, :, 1:2], col(dd[:, TP:2 * TP]), -0.5, 0.5, ALU.mult, ALU.add)
                dve.wait_ge(R[l]["pf"], p + 1)
                ch(nc.vector.tensor_tensor(pos[:, :], ps[:, 1, TP * E:2 * TP * E], ebase[:, :], ALU.add))
                for k in range(K):
                    ch(nc.vector.tensor_tensor(tm8[:, :], pos[:, :], oh[k][:, :], ALU.mult))
                    ch(nc.vector.reduce_sum(posf[:, k * TP:(k + 1) * TP], v3(tm8[:, :], E), axis=AX.X))
                nc.vector.tensor_copy(posi[:, :], posf[:, :]).then_inc(R[l]["pos"], 1)
                ch(nc.vector.reduce_sum(cnt[:, :], mk[:, :].rearrange("p (t e) -> p e t", e=E), axis=AX.X))
                nc.vector.tensor_tensor(run[l][:, :], run[l][:, :], cnt[:, :], ALU.add).then_inc(R[l]["cnt"], 1)

            def table(l):
                F = [tf[:, k * E:(k + 1) * E] for k in range(8)]
                nf, padf, tg, c1, c2, c3 = F[0], F[1], F[2], F[3], F[4], F[5]
                dve.wait_ge(R[l]["pf"], NP + 1)
                ch(nc.vector.tensor_copy(nf, ps[0:1, 1, 0:E]))
                ch(nc.vector.tensor_tensor(padf, nf, ebase[0:1, 0:E], ALU.add))
                ch(nc.vector.tensor_copy(tab[l][:, 2 * NQ:2 * NQ + E], padf))
                ch(nc.vector.tensor_scalar(nf, nf, float(G - 1), None, ALU.add))
                ch(nc.vector.tensor_copy(ti[:, :], nf))
                ch(nc.vector.tensor_scalar(ti[:, :], ti[:, :], G.bit_length() - 1, None, ALU.arith_shift_right))
                ch(nc.vector.tensor_copy(tg, ti[:, :]))
                prev = tg
                for s, nxt in ((1, c1), (2, c2), (4, c3)):
                    ch(nc.vector.tensor_copy(nxt[:, 0:s], prev[:, 0:s]))
                    ch(nc.vector.tensor_tensor(nxt[:, s:E], prev[:, s:E], prev[:, 0:E - s], ALU.add))
                    prev = nxt
                done = tq[:, 0:NQ * E].rearrange("p (q e) -> p q e", e=E)
                past = tq[:, NQ * E:2 * NQ * E].rearrange("p (q e) -> p q e", e=E)

                def over(ap):
                    return ap.rearrange("p (o e) -> p o e", o=1).to_broadcast([1, NQ, E])

                ch(nc.vector.tensor_tensor(done, over(prev), ioq[:, :].rearrange("p (q e) -> p q e", e=E), ALU.is_le))
                ch(nc.vector.tensor_tensor(past, done, over(tg), ALU.mult))
                eq, st, us, of = [tr[:, k * NQ:(k + 1) * NQ] for k in range(4)]
                ch(nc.vector.reduce_sum(eq, done, axis=AX.X))
                ch(nc.vector.reduce_sum(st, past, axis=AX.X))
                ch(nc.vector.tensor_tensor(st.rearrange("p (q o) -> p q o", o=1),
                                           ioq[:, :].rearrange("p (q e) -> p q e", e=E)[:, :, 0:1],
                                           st.rearrange("p (q o) -> p q o", o=1), ALU.subtract))
                ch(nc.vector.tensor_scalar(us, eq, float(E), float(G), ALU.is_lt, ALU.mult))
                ch(nc.vector.tensor_tensor(st, st, us, ALU.mult))
                ch(nc.vector.tensor_scalar(of, eq, float(CAP), None, ALU.mult))
                ch(nc.vector.tensor_tensor(of, of, st, ALU.add))
                ch(nc.vector.tensor_copy(tab[l][:, 0:NQ], of))
                ch(nc.vector.tensor_scalar(eq, eq, float(E - 1), None, ALU.min))
                nc.vector.tensor_copy(tab[l][:, NQ:2 * NQ], eq).then_inc(R[l]["tab"], 1)

            def a_norm(i):
                for j in range(2):
                    for t in range(T):
                        n = (2 * i + j) * T + t
                        last = nc.vector.tensor_scalar(xn[j][:, t * D:(t + 1) * D], xtile(n), mv[:, bass.ds(n * 2, 1)],
                                                       rs[:, bass.ds(n, 1)], ALU.subtract, ALU.mult)
                    last.then_inc(A["xn"], 1)

            def a_parts(i):
                for j in range(2):
                    b = 2 * i + j
                    dve.wait_ge(A["hh"], b + 1)
                    wait(dve, A["agg"], b - 1)
                    pv = ps[:, 2:4, :].rearrange("p k (h d) -> p (k h) d", h=2)
                    nc.vector.tensor_tensor(v3(hl[j][:, :], D), pv[:, :, 0:D], v3(hh[j][:, :], D + 1)[:, :, 0:D], ALU.subtract)
                    nc.vector.tensor_tensor(v3(upd[j][:, :], D), pv[:, :, D:2 * D],
                                            gb[:, :].rearrange("p (o d) -> p o d", o=1).to_broadcast([P, T, D]),
                                            ALU.add).then_inc(A["upd"], 1)

            def a_sum(i):
                for j in range(2):
                    b = 2 * i + j
                    dve.wait_ge(A["agg"], b + 1)
                    av = ps[:, 4:6, :].rearrange("p k (h d) -> p (k h) d", h=2)
                    ch(nc.vector.tensor_scalar(col(deg[j][:, 0:T]), av[:, :, D:D + 1], 1.0, None, ALU.max))
                    ch(nc.vector.reciprocal(deg[j][:, T:2 * T], deg[j][:, 0:T]))
                    for t in range(T):
                        last = nc.vector.scalar_tensor_tensor(upd[j][:, t * D:(t + 1) * D], av[:, t, 0:D],
                                                              deg[j][:, T + t:T + t + 1], upd[j][:, t * D:(t + 1) * D],
                                                              ALU.mult, ALU.add)
                    last.then_inc(A["read"], 1)
                    dve.wait_ge(A["read"], b + 1)
                    ch(nc.vector.scalar_tensor_tensor(xbatch(b), upd[j][:, :], 0.0, xbatch(b), ALU.max, ALU.add), wait_alone)

            def body_a(i, p):
                if i is not None:
                    a_norm(i)
                if p is not None:
                    route_norm(0, p)
                if i is not None:
                    lo_part(A, i)
                if p is not None:
                    route_rows(0, p)
                if i is not None:
                    a_parts(i)
                if p is not None:
                    route_choose(0, p)
                if i is not None:
                    pass
                if p is not None:
                    route_places(0, p)
                if i is not None:
                    a_sum(i)
                    route_stats(0, i)

            pairs_of(dve, body_a, ch, 23)
            table(0)

            def expert_weights(l):
                hw = HID[l]
                dve.wait_ge(s_w[l], 16 * (14, 2)[l])
                w = wx[l][:, :].rearrange("p (e f h) -> p e f h", f=4, h=hw)
                n = E * hw
                if l == 0:
                    dve.wait_ge(s_p, 2)
                    bv = bx[0][:, :].rearrange("p (e c) -> p e c", c=NC[0] + 1)[:, :, 0:NC[0]]
                    ch(nc.vector.tensor_tensor(bv, bv, v3(ps[:, 2, 0:E * NC[0]], NC[0]), ALU.add))
                    for e in range(E):
                        last = nc.vector.tensor_scalar(stage[:, e * hw:(e + 1) * hw], stage[:, e * hw:(e + 1) * hw],
                                                       gT[:, e:e + 1], WS, ALU.mult, ALU.mult)
                    ch(last)
                else:
                    ch(nc.vector.tensor_scalar(stage[:, 0:n], stage[:, 0:n], WS, None, ALU.mult))
                ch(nc.vector.tensor_scalar(stage[:, 4096:4096 + n], stage[:, 4096:4096 + n], WS, None, ALU.mult))
                for f in range(2):
                    src = stage[:, 4096 * f:4096 * f + n].rearrange("p (e h) -> p e h", h=hw)
                    ch(nc.vector.tensor_copy(w[:, :, 2 * f, :], src))
                    last = nc.vector.tensor_tensor(w[:, :, 2 * f + 1, :], src, w[:, :, 2 * f, :], ALU.subtract)
                ch(last)
                mark(nc.vector).then_inc(s_q, 2 - l)

            expert_weights(0)

            def experts(l, steps):
                S, nc_ = M[l], NC[l]
                w = nc_ * G

                def take(n, k4):
                    dve.wait_ge(S["t"], n + 1)
                    wait(dve, S["up"], nc_ // 2 * (n - 1))
                    wait(dve, S[f"sc{k4}"], 32 * rounds(n, k4))
                    ch(nc.vector.tensor_copy(idc[k4][:, :],
                                             gx[k4][:, :].bitcast(U32).rearrange("p (h r) -> p h r", h=2)[:, :, D:D + 1]
                                             .rearrange("p h o -> p (h o)")))
                    nc.vector.tensor_copy(xg[k4 % 2][:, :], bank(6)[:, 0:G].bitcast(F16)).then_inc(S["xg"], 1)

                def hidden(n, k):
                    dve.wait_ge(S["gelu"], nc_ * (n + 1))
                    wait(dve, S["y"], n - 1)
                    ch(nc.vector.tensor_copy(hhi[k][:, 0:w], h32[k][:, 0:w]))
                    nc.vector.tensor_tensor(hlo[k][:, 0:w], h32[k][:, 0:w], hhi[k][:, 0:w], ALU.subtract).then_inc(S["lo"], 1)

                def result(n, k4):
                    dve.wait_ge(S["ytt"], n + 1)
                    wait(dve, S[f"sc{k4}"], 32 * rounds(n, k4))
                    nc.vector.tensor_copy(yrow[k4][:, :], bank(7)[:, 0:G]).then_inc(S["yr"], 1)

                take(0, 0)
                take(1, 1)
                hidden(0, 0)

                def body(n, k4):
                    if not (isinstance(n, int) and n + 2 >= NQ):
                        take(n + 2, (k4 + 2) % 4)
                    if not (isinstance(n, int) and n == 0):
                        result(n - 1, (k4 + 3) % 4)
                    hidden(n + 1, (k4 + 1) % 2)

                groups(dve, body, ch, steps)
                result(NQ - 2, 2)
                result(NQ - 1, 3)

            experts(0, 8)
            expert_weights(1)
            def c_combine(i):
                for j in range(2):
                    b = 2 * i + j
                    dve.wait_ge(C[f"y{j}"], 16 * K * (i + 1))
                    for k in range(K):
                        for t in range(T):
                            n = b * T + t
                            last = nc.vector.scalar_tensor_tensor(
                                xtile(n), yb[j][:, (k * T + t) * D:(k * T + t + 1) * D], wts[:, bass.ds(n * K + k, 1)],
                                xtile(n), ALU.mult, ALU.add)
                        if k == 0:
                            ch(last)
                    last.then_inc(C["comb"], 1)
                wait_alone(dve, (C["comb"], 2 * i + 2))
                statistics(mvc, i * TP)
                nc.vector.tensor_scalar(col(uc[:, :]), v3(mvc[:, :], 2)[:, :, 1:2], EPS, None, ALU.add).then_inc(C["u"], 1)

            def c_norm(i):
                dve.wait_ge(C["r"], i + 1)
                for j in range(2):
                    for t in range(T):
                        n = j * T + t
                        last = nc.vector.tensor_scalar(xn[j][:, t * D:(t + 1) * D], xtile(i * TP + n),
                                                       mvc[:, 2 * n:2 * n + 1], rc[:, n:n + 1], ALU.subtract, ALU.mult)
                    last.then_inc(C["xn"], 1)

            def c_scores(b, j):
                wait_alone(dve, (C["proj"], b + 1), (C["conv"], b + 1))
                r_ = rowb[j]
                M_, s1, m_ = r_[:, 2 * T:3 * T], r_[:, 3 * T:4 * T], r_[:, 4 * T:5 * T]
                for t in range(T):
                    last = nc.vector.tensor_tensor_reduce(
                        out=tt(j, t), in0=bank(7), in1=adjF[j][:, t * N:(t + 1) * N].bitcast(BF16), scale=1.0,
                        scalar=-3.0e38, op0=ALU.add, op1=ALU.max, accum_out=M_[:, t:t + 1])
                ch(last)
                dve.wait_ge(C["wh"], b + 1)
                sv = ps[:, 2:4, :].rearrange("p k (h d) -> p (k h) d", h=2)
                ch(nc.vector.tensor_copy(col(s1), sv[:, :, D:D + 1]))
                ch(nc.vector.tensor_tensor(M_, M_, s1, ALU.add))
                ch(nc.vector.scalar_tensor_tensor(m_, M_, SLOPE, M_, ALU.mult, ALU.max))
                nc.vector.tensor_tensor(r_[:, 0:T], s1, m_, ALU.subtract)
                nc.vector.scalar_tensor_tensor(r_[:, T:2 * T], s1, SLOPE, m_, ALU.mult, ALU.subtract).then_inc(C["bias"], 1)

            def c_attend(b, j):
                def take_max(t):
                    q = 4 * b + t
                    dve.wait_ge(C["e"], q + 1)
                    wait(dve, C["ptr"], q - 1)
                    nc.vector.tensor_tensor(part(2, t), part(0, t), part(1, t), ALU.max).then_inc(C["p"], 1)

                def evict(t):
                    dve.wait_ge(C["av"], 4 * b + t + 1)
                    rec = rowb[j][:, 5 * T + t:5 * T + t + 1]
                    ch(nc.vector.reciprocal(rec, ps[:, 6, D:D + 1]))
                    nc.vector.tensor_scalar(hpb[j][:, t * D:(t + 1) * D], ps[:, 6, 0:D], rec, None, ALU.mult
                                            ).then_inc(C["fin"], 1)

                for t in range(T):
                    take_max(t)
                    if t >= 2:
                        evict(t - 2)
                evict(T - 2)
                evict(T - 1)
                dve.wait_ge(C["fin"], 4 * b + 4)
                nc.vector.tensor_scalar(mnb[j][:, :], hpb[j][:, :], 0.0, None, ALU.min).then_inc(C["mn"], 1)

            def c_add(b, j):
                ch(nc.vector.scalar_tensor_tensor(xbatch(b), hpb[j][:, :], 0.0, xbatch(b), ALU.max, ALU.add))
                dve.wait_ge(C["ex"], b + 1)
                ch(nc.vector.scalar_tensor_tensor(xbatch(b), mnb[j][:, :], -1.0, xbatch(b), ALU.add, ALU.add), wait_alone)

            def body_c(i, p):
                if i is not None:
                    c_combine(i)
                if p is not None:
                    route_norm(1, p)
                if i is not None:
                    c_norm(i)
                if i is not None:
                    lo_part(C, i)
                if p is not None:
                    route_rows(1, p)
                if p is not None:
                    route_choose(1, p)
                if i is not None:
                    c_scores(2 * i, 0)
                if p is not None:
                    route_places(1, p)
                if i is not None:
                    c_attend(2 * i, 0)
                    c_scores(2 * i + 1, 1)
                    c_add(2 * i, 0)
                    c_attend(2 * i + 1, 1)
                    c_add(2 * i + 1, 1)
                    route_stats(1, i)

            pairs_of(dve, body_c, ch, 38)
            table(1)
            experts(1, 8)

            def add_up(i):
                for j in range(2):
                    b = 2 * i + j
                    dve.wait_ge(Z[f"y{j}"], 16 * K * (i + 1))
                    ch(nc.vector.tensor_tensor(xbatch(b), xbatch(b), yb[j][:, 0:N], ALU.add))
                    nc.vector.tensor_tensor(xbatch(b), xbatch(b), yb[j][:, N:2 * N], ALU.add).then_inc(Z["add"], 1)

            with dve.Fori(0, NP) as i:
                ch.enter(i, 0, 2)
                add_up(i)
            ch.leave(NP)


_INS = ['x', 'adj', 'L0_gnn_W_msg', 'L0_gnn_W_upd', 'L0_gnn_bias', 'L0_ffn_Wr', 'L0_ffn_br', 'L0_ffn_ln_g', 'L0_ffn_ln_b',
        'L0_ffn_W1', 'L0_ffn_b1', 'L0_ffn_W2', 'L0_ffn_b2', 'L1_gnn_W', 'L1_gnn_a', 'L1_ffn_Wg', 'L1_ffn_bg', 'L1_ffn_W1',
        'L1_ffn_b1', 'L1_ffn_W2', 'L1_ffn_b2']


def kernel(**inputs):
    import concourse.bacc as _bacc
    from concourse.bass_utils import run_bass_kernel_spmd as _run

    nc = _bacc.Bacc("TRN2", target_bir_lowering=False, num_devices=1)
    arrays, args = {}, []

    def give(name, a):
        arrays[name] = a
        args.append(nc.dram_tensor(name, a.shape, mybir.dt.from_np(a.dtype), kind="ExternalInput").ap())

    for name in _INS:
        give(f"in_{name}_dram", np.ascontiguousarray(inputs[name]))
    give("c_identf", np.eye(P, dtype=np.float32))
    give("c_identh", np.eye(P, dtype=np.float16))
    give("c_lower", np.concatenate([np.triu(np.ones((P, P), np.float16), 1), np.ones((P, P), np.float16)], 1))
    e8 = np.tile(np.arange(E, dtype=np.float32), (P, TP))
    give("c_iota8", np.stack([e8, e8 * CAP]))
    k, i, t, p = np.meshgrid(np.arange(K), np.arange(NP), np.arange(TP), np.arange(P), indexing="ij")
    give("c_ids", np.ascontiguousarray((k * TOK + (i * TP + t) * P + p).transpose(3, 1, 0, 2).reshape(P, -1).astype(np.uint32)))
    give("c_iotaq", np.repeat(np.arange(NQ, dtype=np.float32), E)[None])
    args.append(nc.dram_tensor("out_0_dram", (NB, N, D), F32, kind="ExternalOutput").ap())
    build(nc, *args)
    r = _run(nc, [arrays], core_ids=[0])
    return r.results[0]["out_0_dram"]
```

```python
import numpy as np
import concourse.bass as bass
from concourse import mybir
from contextlib import ExitStack

P = 128
NB, N, D = 16, 512, 128
T = N // P
NT = NB * T
NP = NB // 2
TP = 2 * T
TOK = NB * N
E, K = 8, 2
HID = (512, 256)
G = 512
H = G // P
NQ = TOK * K // G + E - 1
CAP = TOK + G
ROW = 288
NOWHERE = 1 << 20
NL = (NQ - 7) // 4
assert NQ == 4 * NL + 7 and NL == E
EPS = 1e-5
SLOPE = 0.2
NEG = -float(2 ** 53)
WS = 64.0

F32, F16, BF16 = mybir.dt.float32, mybir.dt.float16, mybir.dt.bfloat16
I32, U32 = mybir.dt.int32, mybir.dt.uint32
ALU = mybir.AluOpType
ACT = mybir.ActivationFunctionType
AX = mybir.AxisListType


class Chain:

    def __init__(self, eng, sem):
        self.eng, self.sem, self.base, self.k = eng, sem, 0, 0

    def __call__(self, ins, alone=None):
        self.k += 1
        ins.then_inc(self.sem, 1)
        if alone:
            alone(self.eng, (self.sem, self.base + self.k))
        else:
            self.eng.wait_ge(self.sem, self.base + self.k)

    def enter(self, i, first, steps):
        self.before, self.steps = self.base + self.k, steps
        self.base, self.k = (i - first) * steps + self.before, 0

    def leave(self, rounds):
        assert self.k == self.steps, f"CHAIN {self.k} for {self.steps}"
        self.base, self.k = self.before + rounds * self.steps, 0


def build(nc, x, adj, W_msg, W_upd, g_bias, Wr, br, ln_g, ln_b, W1a, b1a, W2a, b2a,
          W, a, Wg, bg, W1b, b1b, W2b, b2b, identf, identh, lower, iota8, ids, iotaq, out):
    ctx = ExitStack()
    with ctx:
        def sb(name, shape, dt=F32):
            return ctx.enter_context(nc.sbuf_tensor(name, shape, dt))

        def sem(name):
            return ctx.enter_context(nc.semaphore(name))

        def sems(prefix, names):
            return {n: sem(f"{prefix}_{n}") for n in names.split()}

        slots = [nc.dram_tensor(f"slots{l}", [E * CAP + G, ROW // 2], U32).ap() for l in range(2)]
        ys = [nc.dram_tensor(f"ys{l}", [K * TOK, D], F32).ap() for l in range(2)]

        xs = sb("xs", [P, NT * D])
        ps = ctx.enter_context(nc.psum_tensor("ps", [P, 8, 512], F32))
        idf = sb("idf", [P, P])
        idh = sb("idh", [P, P], F16)
        low = sb("low", [P, 2 * P], F16)
        io8 = sb("io8", [P, TP * E])
        ebase = sb("ebase", [P, TP * E])
        idt = sb("idt", [P, NP * K * TP], U32)
        ioq = sb("ioq", [1, NQ * E])
        mhalf = sb("mhalf", [P, 2 * TP])
        zt = sb("zt", [P, 64])
        cells = iter(range(64))

        stage = sb("stage", [P, 8192])
        wA = [sb(f"wA{k}", [P, 2 * D], F16) for k in range(2)]
        wC = [sb(f"wC{k}", [P, D + 2], F16) for k in range(2)]
        wS = [sb(f"wS{k}", [P, P], F16) for k in range(2)]
        wR = [[sb(f"wR{l}{k}", [P, E], F16) for k in range(2)] for l in range(2)]
        wx = [sb(f"wx{l}", [P, E * 4 * HID[l]], F16) for l in range(2)]
        NC = [h // P for h in HID]
        bx = [sb(f"bx{l}", [P, E * (NC[l] + 1)]) for l in range(2)]
        gb = sb("gb", [P, D])
        rb = [sb(f"rb{l}", [P, E]) for l in range(2)]
        gT = sb("gT", [P, E])
        g64 = sb("g64", [P, E])
        bT = sb("bT", [P, E])
        acol = sb("acol", [P, 2])

        adjI = [sb(f"adjI{j}", [P, T * N], I32) for j in range(2)]
        adjF = [sb(f"adjF{j}", [P, T * N], F16) for j in range(2)]
        xn = [sb(f"xn{j}", [P, T * D]) for j in range(2)]
        xTh = [sb(f"xTh{j}", [P, N], F16) for j in range(2)]
        xTl = [sb(f"xTl{j}", [P, N], F16) for j in range(2)]
        hh = [sb(f"hh{j}", [P, T * (D + 1)], F16) for j in range(2)]
        hl = [sb(f"hl{j}", [P, T * D], F16) for j in range(2)]
        upd = [sb(f"upd{j}", [P, T * D]) for j in range(2)]
        deg = [sb(f"deg{j}", [P, 2 * T]) for j in range(2)]
        whE = [sb(f"whE{j}", [P, T * (D + 1)]) for j in range(2)]
        rowb = [sb(f"rowb{j}", [P, 6 * T]) for j in range(2)]
        st6 = sb("st6", [P, TP * 6])
        mvc = sb("mvc", [P, TP * 2])
        uc = sb("uc", [P, TP])
        rc = sb("rc", [P, TP])
        nm = sb("nm", [P, TP])
        mvr = sb("mvr", [P, TP * 2])
        ur = sb("ur", [P, 2 * TP])
        rr = sb("rr", [P, 2 * TP])
        cinv = sb("cinv", [P, TP])
        xr = sb("xr", [P, TP * D])
        smf, wcf, Wf = xr[:, 0:2 * D + 16], xr[:, 3 * D:4 * D + 2], xr[:, 5 * D:6 * D]
        eb = sb("eb", [P, 6 * G])
        rows = [sb("rows", [P, K * TP * ROW], F16), eb[:, 0:K * TP * ROW // 2].bitcast(F16)]
        xTr = sb("xTr", [P, TP * 2 * P], F16)
        lg = sb("lg", [P, TP * E])
        mx8 = sb("mx8", [P, TP * E])
        ix8 = sb("ix8", [P, TP * E], U32)
        ixf = sb("ixf", [P, TP * E])
        oh = [sb(f"oh{k}", [P, TP * E]) for k in range(K)]
        mk = sb("mk", [P, TP * E], F16)
        run = [sb(f"run{l}", [P, E], F16) for l in range(2)]
        cnt = sb("cnt", [P, E])
        dd = sb("dd", [P, 2 * TP])
        pos = sb("pos", [P, TP * E])
        tm8 = sb("tm8", [P, TP * E])
        posf = sb("posf", [P, K * TP])
        posi = [sb(f"posi{w}", [P, K * TP], U32) for w in range(2)]
        padr = sb("padr", [P, H * ROW], F16)
        tf = sb("tf", [1, 8 * E])
        ti = sb("ti", [1, E], I32)
        tq = sb("tq", [1, 2 * NQ * E])
        tr = sb("tr", [1, 4 * NQ])
        tab = [sb(f"tab{l}", [1, 2 * NQ + E], I32) for l in range(2)]
        gx = [rows[0][:, k * H * ROW:(k + 1) * H * ROW] for k in range(4)]
        xg = [xTr[:, k * 2 * G:(k + 1) * 2 * G] for k in range(2)]
        yT = [xr[:, k * G:(k + 1) * G] for k in range(2)]
        idg = [sb(f"idg{k}", [P, 2 * H], U32) for k in range(4)]
        idc = [sb(f"idc{k}", [P, H], U32) for k in range(4)]
        bcur = [sb(f"bcur{k}", [P, NC[0] + 1]) for k in range(4)]
        h32 = [eb[:, k * 2 * G:(k + 1) * 2 * G] for k in range(2)]
        hhi = [adjI[0][:, :].bitcast(F16)[:, k * 4 * G:(k + 1) * 4 * G] for k in range(2)]
        hlo = [adjF[k][:, 0:4 * G] for k in range(2)]
        yrows = eb[:, 4 * G:6 * G]
        yrow = [yrows[:, 0:G], yrows[:, G:2 * G], upd[0], upd[1]]
        yb = h32
        hpb = upd
        mnb = [yrows[:, j * T * D:(j + 1) * T * D] for j in range(2)]

        s_c = sem("s_c")
        s_x = [sem(f"s_x{q}") for q in range(4)]
        s_w = [sem(f"s_w{l}") for l in range(2)]
        s_p = sem("s_p")
        s_q = sem("s_q")
        s_ch = sem("s_ch")
        s_m = sem("s_m")
        s_always = sem("s_always")
        s_out = sem("s_out")
        s_cb = sem("s_cb")
        A = sems("A", "adj0 adj1 conv u r nm xn tr hi lo proj hh upd agg read fin")
        C = sems("C", "adj0 adj1 y0 y1 conv comb u r nm xn tr hi lo proj wh sum bias e p ptr pt av fin mn ex")
        R = [sems(f"R{l}", "u r xr hi rows t x lg mk d th pf pos copy sc0 sc1 cnt tab pad") for l in range(2)]
        M = [sems(f"M{l}", "ld0 ld1 ld2 ld3 t xg up bc gelu lo y yt ytt yr sc0 sc1 sc2 sc3") for l in range(2)]
        Z = sems("Z", "y0 y1 y2 y3 add")
        WP = [sems(f"W{l}", "g hi lo") for l in range(2)]

        block = ctx.enter_context(nc.Block())

        def bank(k):
            return ps[:, k, :]

        def v3(ap, k):
            return ap.rearrange("p (t k) -> p t k", k=k)

        def col(ap):
            return ap.rearrange("p (t o) -> p t o", o=1)

        def rows_of(w, k, lo, hi):
            return rows[w][:, k * TP * ROW:(k + 1) * TP * ROW].rearrange("p (t r) -> p t r", r=ROW)[:, :, lo:hi]

        def wait(eng, semaphore, value):
            if not isinstance(value, int) or value > 0:
                eng.wait_ge(semaphore, value)

        def wait_alone(eng, *pairs):
            pairs = [(s, v if isinstance(v, int) else eng.to_reg(v)) for s, v in pairs if not isinstance(v, int) or v > 0]
            eng.wait_ge(s_always, 1)
            for s, v in pairs:
                eng.wait_ge(s, v)

        def mark(eng):
            c = next(cells)
            return eng.memset(zt[:, c:c + 1], 0.0)

        def xbatch(b):
            return xs[:, bass.ds(b * (T * D), T * D)]

        def xtile(n):
            return xs[:, bass.ds(n * D, D)]

        def tt(j, t):
            return stage[:, (j * T + t) * N:(j * T + t + 1) * N]

        def part(k, t):
            return stage[:, 4096 + (2 * k + t % 2) * N:4096 + (2 * k + t % 2 + 1) * N]

        def zb(m):
            return stage[:, m * 2 * G:(m + 1) * 2 * G]

        def av_bank(t):
            return (6, 0)[t % 2]

        def weight_parts(l, e):
            hw = HID[l]
            for f in range(2):
                src = stage[:, bass.ds(e * hw + 4096 * f, hw)]
                factor = g64[:, bass.ds(e, 1)] if l == 0 and f == 0 else WS
                yield src, factor, [wx[l][:, bass.ds(e * (4 * hw) + (2 * f + k) * hw, hw)] for k in range(2)]

        def more(i):
            return i is not None and not (isinstance(i, int) and i == NP - 1)

        def pairs_of(eng, body, chain=None, steps=0, ahead=0):
            body(0, None)
            body(1, 0)
            with eng.Fori(2, NP - ahead) as i:
                if chain:
                    chain.enter(i, 2, steps)
                body(i, i - 1)
            if chain:
                chain.leave(NP - ahead - 2)
            if ahead:
                body(NP - 1, NP - 2)
            body(None, NP - 1)

        def pairs_by_two(eng, body, chain=None, steps=0):
            body(0, None, 0)
            body(1, 0, 0)
            with eng.Fori(1, NP // 2 - 1) as i:
                if chain:
                    chain.enter(i, 1, steps)
                body(2 * i, 2 * i - 1, 1)
                body(2 * i + 1, 2 * i, 0)
            if chain:
                chain.leave(NP // 2 - 2)
            body(NP - 2, NP - 3, 1)
            body(NP - 1, NP - 2, 0)
            body(None, NP - 1, 1)

        def groups(eng, body, chain=None, steps=0, beside=None):
            for n in range(5):
                body(n, n % 4)
            with eng.Fori(1, 1 + NL) as i:
                if chain:
                    chain.enter(i, 1, steps)
                if beside:
                    beside(i - 1)
                for d in range(4):
                    body(4 * i + 1 + d, (1 + d) % 4)
            if chain:
                chain.leave(NL)
            body(NQ - 2, (NQ - 2) % 4)

        def hbuf(q):
            return h32[q // 2][:, (q % 2) * G:(q % 2 + 1) * G]

        def rounds(n, k4):
            return n // 4 if isinstance(n, int) else (n - k4) // 4

        @block.sync
        def _(sp):
            def slow(dst, src, s):
                sp.dma_start(dst, src, allow_slow_non_contiguous=True).then_inc(s, 16)

            def load_x(q):
                n = NT // 4
                sp.dma_start(xs[:, q * n * D:(q + 1) * n * D].rearrange("p (n d) -> p n d", d=D),
                             x[q * NB // 4:(q + 1) * NB // 4].rearrange("b (t p) d -> p (b t) d", p=P)).then_inc(s_x[q], 16)

            load_x(0)
            sp.dma_start(smf[:, 0:D], W_msg).then_inc(s_c, 16)
            sp.dma_start(smf[:, D:2 * D], W_upd).then_inc(s_c, 16)
            sp.dma_start(smf[:, 2 * D:2 * D + 8], Wr).then_inc(s_c, 16)
            sp.dma_start(smf[:, 2 * D + 8:2 * D + 16], Wg).then_inc(s_c, 16)
            sp.dma_start(idf[:, :], identf).then_inc(s_c, 16)
            sp.dma_start(idh[:, :], identh).then_inc(s_c, 16)
            sp.dma_start(low[:, :], lower).then_inc(s_c, 16)
            sp.dma_start(io8[:, :], iota8[0]).then_inc(s_c, 16)
            sp.dma_start(ebase[:, :], iota8[1]).then_inc(s_c, 16)
            sp.dma_start(idt[:, :], ids).then_inc(s_c, 16)
            sp.dma_start(ioq[:, :], iotaq).then_inc(s_c, 16)
            sp.dma_start(Wf[:, :], W).then_inc(s_c, 16)
            sp.dma_start(gb[:, :], g_bias.partition_broadcast(P)).then_inc(s_c, 16)
            sp.dma_start(rb[0][:, :], br.partition_broadcast(P)).then_inc(s_c, 16)
            sp.dma_start(rb[1][:, :], bg.partition_broadcast(P)).then_inc(s_c, 16)
            slow(acol[:, :], a.rearrange("(k o) one -> o (k one)", k=2), s_c)

            def load_adj(S, i):
                for j in range(2):
                    wait(sp, S["conv"], 2 * i + j - 1)
                    sp.dma_start(adjI[j][:, :].rearrange("p (t n) -> p t n", n=N),
                                 adj[bass.ds(2 * i + j, 1)].rearrange("o (t p) n -> p (o t) n", p=P)
                                 ).then_inc(S[f"adj{j}"], 16)

            load_adj(A, 0)
            for q in range(1, 4):
                load_x(q)
            for h in range(2):
                sp.dma_start(stage[:, 2048 * h:2048 * (h + 1)].rearrange("p (e h) -> p e h", h=HID[0]),
                             W1a[4 * h:4 * h + 4].rearrange("e d h -> d e h")).then_inc(s_w[0], 16)
                sp.dma_start(stage[:, 4096 + 2048 * h:4096 + 2048 * (h + 1)].rearrange("p (e c d) -> p e c d", c=4, d=D),
                             W2a[4 * h:4 * h + 4].rearrange("e (c p) d -> p e c d", p=P)).then_inc(s_w[0], 16)
            slow(gT[:, :], ln_g.rearrange("e d -> d e"), s_w[0])
            slow(bT[:, :], ln_b.rearrange("e d -> d e"), s_w[0])
            for l, b1, b2 in ((0, b1a, b2a), (1, b1b, b2b)):
                v = bx[l][:, :].rearrange("p (e c) -> p e c", c=NC[l] + 1)
                for c in range(NC[l]):
                    slow(v[:, :, c:c + 1], b1[:, c * P:(c + 1) * P].rearrange("e (p o) -> p e o", o=1), s_w[0])
                slow(v[:, :, NC[l]:NC[l] + 1], b2.rearrange("e (p o) -> p e o", o=1), s_w[0])
            load_adj(A, 1)
            with sp.Fori(2, NP) as i:
                load_adj(A, i)

            def pads(l):
                sp.wait_ge(R[l]["tab"], 1)
                sp.wait_ge(s_m, 2)
                for e in range(E + 1):
                    at = E * CAP
                    if e < E:
                        at = sp.value_load(tab[l][0:1, 2 * NQ + e:2 * NQ + e + 1], min_val=0, max_val=E * CAP)
                    sp.dma_start(slots[l][bass.ds(at, G), :].rearrange("(p h) r -> p (h r)", h=H), padr[:, :].bitcast(U32)
                                 ).then_inc(R[l]["pad"], 16)

            def fetch(l, n, k):
                S = M[l]
                wait(sp, S["xg"], n - 3)
                at = sp.value_load(tab[l][0:1, bass.ds(n, 1)], min_val=0, max_val=E * CAP)
                sp.dma_start(gx[k][:, :].bitcast(U32), slots[l][bass.ds(at, G), :].rearrange("(p h) r -> p (h r)", h=H)
                             ).then_inc(S[f"ld{k}"], 16)

            def fetch_first(l):
                for w in range(2 - l):
                    sp.wait_ge(R[l][f"sc{w}"], 16 * K * NT // (2 - l))
                sp.wait_ge(R[l]["pad"], 16 * (E + 1))
                for n in range(4):
                    fetch(l, n, n)

            def fetch_others(l):
                with sp.Fori(1, NQ // 4) as i:
                    for k in range(4):
                        fetch(l, 4 * i + k, k)
                for n in range(NQ // 4 * 4, NQ):
                    fetch(l, n, n % 4)

            def scattered(l):
                for k in range(4):
                    sp.wait_ge(M[l][f"sc{k}"], 16 * H * len(range(k, NQ, 4)))

            def load_y(l, S, b, j, into, buffers):
                wait(sp, S[("comb", "add")[l]], K * (b - buffers + 1))
                for k in range(K):
                    sp.dma_start(into[:, k * N:(k + 1) * N].rearrange("p (t d) -> p t d", d=D),
                                 ys[l].rearrange("(n p) d -> p n d", p=P)[:, bass.ds(b * T + k * NT, T), :]
                                 ).then_inc(S[f"y{j}"], 16)

            pads(0)
            fetch_first(0)
            sp.wait_ge(WP[0]["lo"], E)
            sp.wait_ge(s_p, 2)
            sp.dma_start(stage[:, 0:2048].rearrange("p (e h) -> p e h", h=HID[1]), W1b.rearrange("e d h -> d e h")).then_inc(s_w[1], 16)
            sp.dma_start(stage[:, 4096:6144].rearrange("p (e c d) -> p e c d", c=2, d=D),
                         W2b.rearrange("e (c p) d -> p e c d", p=P)).then_inc(s_w[1], 16)
            fetch_others(0)
            sp.wait_ge(A["conv"], NB)
            scattered(0)

            def graph1(i):
                for j in range(2):
                    load_y(0, C, 2 * i + j, j, yb[j], 2)

            graph1(0)
            load_adj(C, 0)
            load_adj(C, 1)
            graph1(1)
            with sp.Fori(2, NP) as i:
                graph1(i)
                load_adj(C, i)
            pads(1)
            fetch_first(1)
            fetch_others(1)
            scattered(1)

            for m in range(4):
                load_y(1, Z, m, m, zb(m), 4)
            with sp.Fori(1, NB // 4) as i:
                for m in range(4):
                    load_y(1, Z, 4 * i + m, m, zb(m), 4)

        @block.gpsimd
        def _(pool):
            mark(nc.gpsimd).then_inc(s_always, 1)
            nc.gpsimd.memset(mhalf[:, :], -0.5).then_inc(s_m, 1)
            pool.wait_ge(s_m, 2)

            def masks(S, i, used, add, mult, dt):
                for j in range(2):
                    b = 2 * i + j
                    wait_alone(pool, (S[f"adj{j}"], 16 * i + 16), (S[used], b - 1))
                    nc.gpsimd.tensor_scalar(adjF[j][:, :].bitcast(dt), adjI[j][:, :], add, mult, ALU.add, ALU.mult
                                            ).then_inc(S["conv"], 1)

            def norm_power(S, i):
                pool.wait_ge(S["u"], i + 1)
                nc.gpsimd.tensor_tensor(rc[:, :], uc[:, :], mhalf[:, 0:TP], ALU.pow).then_inc(S["r"], 1)

            def route_power(l, p):
                pool.wait_ge(R[l]["u"], p + 1)
                n = 2 * TP if l == 0 else TP
                nc.gpsimd.tensor_tensor(rr[:, 0:n], ur[:, 0:n], mhalf[:, 0:n], ALU.pow).then_inc(R[l]["r"], 1)

            def scatter(l, p, first, end, w=0):
                copied = [(R[0]["copy"], p + 1)] if l == 0 and end == K * TP else []
                wait_alone(pool, (R[l]["rows"], p + 1), (R[l]["pos"], p + 1), *copied)
                for c in range(first, end):
                    nc.gpsimd.indirect_dma_start(
                        slots[l], bass.IndirectOffsetOnAxis(ap=posi[w][:, c:c + 1], axis=0),
                        rows[w][:, c * ROW:(c + 1) * ROW].bitcast(U32), None).then_inc(R[l][f"sc{w}"], 16)

            def body_a(i, p, w):
                if more(i):
                    norm_power(A, i + 1)
                    masks(A, i + 1, "agg", 0.0, 1.0, F16)
                if p is not None:
                    scatter(0, p, 0, 4, w)
                if i is not None:
                    route_power(0, i)
                if p is not None:
                    scatter(0, p, 4, K * TP, w)

            def body_c(i, p):
                if p is not None:
                    route_power(1, p)
                if i is not None:
                    masks(C, i, "bias", -1.0, -NEG, BF16)
                if p is not None:
                    scatter(1, p, 0, TP + 1)
                if more(i):
                    norm_power(C, i + 1)
                if p is not None:
                    scatter(1, p, TP + 1, K * TP)

            def put_back(l, n, k):
                S = M[l]
                wait_alone(pool, (S["yr"], n + 1))
                for h in range(H):
                    nc.gpsimd.indirect_dma_start(
                        ys[l], bass.IndirectOffsetOnAxis(ap=idc[k][:, h:h + 1], axis=0), yrow[k][:, h * D:(h + 1) * D], None,
                        bounds_check=K * TOK - 1, oob_is_err=False).then_inc(S[f"sc{k}"], 16)

            norm_power(A, 0)
            masks(A, 0, "agg", 0.0, 1.0, F16)
            pairs_by_two(pool, body_a)
            with pool.Fori(0, NQ // 4) as i:
                for k in range(4):
                    put_back(0, 4 * i + k, k)
            for n in range(NQ // 4 * 4, NQ):
                put_back(0, n, n % 4)
            norm_power(C, 0)
            pairs_of(pool, body_c, ahead=1)
            with pool.Fori(0, NQ // 4) as i:
                for k in range(4):
                    put_back(1, 4 * i + k, k)
            for n in range(NQ // 4 * 4, NQ):
                put_back(1, n, n % 4)

        @block.scalar
        def _(act):
            def weights_hi(l, e):
                if l == 1:
                    act.wait_ge(s_w[1], 16 * 2)
                for src, factor, (hi, lo) in weight_parts(l, e):
                    last = nc.scalar.activation(hi, src, ACT.Copy, scale=factor)
                last.then_inc(WP[l]["hi"], 1)

            def norm(S, i):
                wait_alone(act, (S["nm"], i + 1))
                for j in range(2):
                    for t in range(T):
                        n = j * T + t
                        last = nc.scalar.activation(xn[j][:, t * D:(t + 1) * D], xtile(i * TP + n), ACT.Identity,
                                                    bias=nm[:, n:n + 1], scale=rc[:, n:n + 1])
                    last.then_inc(S["xn"], 1)

            def graph_hi(S, i):
                for j in range(2):
                    b = 2 * i + j
                    wait(act, S["proj"], b - 1)
                    act.wait_ge(S["tr"], b + 1)
                    nc.scalar.activation(xTh[j][:, :], bank((0, 6)[j]), ACT.Copy).then_inc(S["hi"], 1)

            def route_hi(l, p, w=0):
                wait(act, R[l][f"sc{w}"], 16 * K * TP * ((p - w) // 2 if l == 0 else p))
                act.wait_ge(R[l]["xr"], p + 1)
                nc.scalar.activation(rows_of(w, 0, 0, D), v3(xr[:, :], D), ACT.Copy).then_inc(R[l]["hi"], 1)

            def route_x(l, p):
                for j in range(2):
                    act.wait_ge(R[l]["t"], 2 * p + j + 1)
                    nc.scalar.activation(xTr[:, j * 8 * P:(j + 1) * 8 * P], bank((0, 6)[j]).bitcast(F16), ACT.Copy
                                         ).then_inc(R[l]["x"], 1)

            def route_tanh(p):
                act.wait_ge(R[0]["d"], p + 1)
                nc.scalar.activation(dd[:, TP:2 * TP], dd[:, 0:TP], ACT.Tanh, scale=0.5).then_inc(R[0]["th"], 1)

            def halves(lo, hi):
                return ps[:, lo:lo + 2, :].rearrange("p k (h d) -> p (k h) d", h=2)[:, :, 0:hi]

            def hh_part(b, j):
                wait(act, A["agg"], b - 1)
                act.wait_ge(A["proj"], b + 1)
                nc.scalar.activation(v3(hh[j][:, :], D + 1)[:, :, 0:D], halves(2, D), ACT.Copy).then_inc(A["hh"], 1)

            def body_a(i, p, w):
                if i is not None:
                    hh_part(2 * i, 0)
                if p is not None:
                    route_hi(0, p, w)
                if i is not None:
                    hh_part(2 * i + 1, 1)
                if p is not None:
                    route_x(0, p)
                    route_tanh(p)
                    act.wait_ge(R[0]["rows"], p + 1)
                    nc.scalar.activation(rows_of(w, 1, 0, 2 * D), rows_of(w, 0, 0, 2 * D), ACT.Copy).then_inc(R[0]["copy"], 1)
                    if isinstance(p, int) and p == 0:
                        act.wait_ge(WP[0]["g"], 1)
                    weights_hi(0, p)
                if more(i):
                    norm(A, i + 1)
                    graph_hi(A, i + 1)

            norm(A, 0)
            graph_hi(A, 0)
            pairs_by_two(act, body_a)

            def experts(l):
                S, nc_ = M[l], NC[l]

                def hidden(n, k4):
                    wait(act, S["yt"], n - 3)
                    e = act.value_load(tab[l][0:1, bass.ds(n + NQ, 1)], min_val=0, max_val=E - 1)
                    nc.scalar.activation(bcur[k4][:, 0:nc_ + 1], bx[l][:, bass.ds(e * (nc_ + 1), nc_ + 1)], ACT.Copy
                                         ).then_inc(S["bc"], 1)
                    act.wait_ge(S["bc"], n + 1)
                    for c in range(nc_):
                        q = (nc_ * k4 + c) % 4
                        wait(act, S["lo"], nc_ * n + c - 3)
                        act.wait_ge(S["up"], nc_ * n + c + 1)
                        nc.scalar.activation(hbuf(q), bank(q), ACT.Gelu, bias=bcur[k4][:, c:c + 1], scale=1.0 / WS
                                             ).then_inc(S["gelu"], 1)

                def result(n, k4):
                    act.wait_ge(S["y"], n + 1)
                    wait(act, S["ytt"], n - 1)
                    nc.scalar.activation(yT[k4 % 2], bank(4 + k4 % 2), ACT.Identity,
                                         bias=bcur[k4][:, nc_:nc_ + 1], scale=1.0 / WS).then_inc(S["yt"], 1)

                act.wait_ge(R[l]["tab"], 1)
                act.wait_ge(s_q, 2)
                hidden(0, 0)

                def body(n, k4):
                    if not (isinstance(n, int) and n == 0):
                        result(n - 1, (k4 + 3) % 4)
                    hidden(n + 1, (k4 + 1) % 4)

                groups(act, body, beside=(lambda e: weights_hi(1, e)) if l == 0 else None)
                result(NQ - 2, (NQ - 2) % 4)
                result(NQ - 1, (NQ - 1) % 4)

            experts(0)

            def wh_part(b, j):
                wait(act, C["av"], 4 * b - 4)
                act.wait_ge(C["proj"], b + 1)
                nc.scalar.activation(v3(whE[j][:, :], D + 1)[:, :, 0:D], halves(2, D), ACT.Copy).then_inc(C["wh"], 1)

            def copy_pt(b, t):
                q = 4 * b + t
                act.wait_ge(C["ptr"], q + 1)
                wait(act, C["av"], q - 1)
                nc.scalar.activation(part(3, t), bank(4 + t % 2), ACT.Copy).then_inc(C["pt"], 1)

            def elu_exp(b, j):
                act.wait_ge(C["fin"], 4 * b + 4)
                nc.scalar.activation(mnb[j][:, :], hpb[j][:, :], ACT.Relu, scale=-1.0).then_inc(C["mn"], 1)
                act.wait_ge(C["mn"], b + 1)
                nc.scalar.activation(mnb[j][:, :], mnb[j][:, :], ACT.Exp, scale=-1.0).then_inc(C["ex"], 1)

            def exps(b, j, t):
                if t == 0:
                    act.wait_ge(C["bias"], b + 1)
                wait(act, C["p"], 4 * b + t - 1)
                nc.scalar.activation(part(0, t), tt(j, t), ACT.Exp, bias=rowb[j][:, t:t + 1])
                nc.scalar.activation(part(1, t), tt(j, t), ACT.Exp, bias=rowb[j][:, T + t:T + t + 1],
                                     scale=SLOPE).then_inc(C["e"], 1)

            def body_c(i, p):
                if i is not None:
                    wh_part(2 * i, 0)
                if p is not None:
                    route_hi(1, p)
                    route_x(1, p)
                if i is not None:
                    for q in range(2 * T):
                        exps(2 * i + q // T, q // T, q % T)
                        if q >= 2:
                            copy_pt(2 * i + (q - 2) // T, (q - 2) % T)
                        if q == 1:
                            wh_part(2 * i + 1, 1)
                    copy_pt(2 * i + 1, T - 2)
                    copy_pt(2 * i + 1, T - 1)
                    elu_exp(2 * i, 0)
                    elu_exp(2 * i + 1, 1)
                if more(i):
                    norm(C, i + 1)
                    graph_hi(C, i + 1)

            norm(C, 0)
            graph_hi(C, 0)
            pairs_of(act, body_c, ahead=1)
            experts(1)

            with act.Fori(0, NB) as b:
                act.wait_ge(Z["add"], K * (b + 1))
                act.dma_start(out[bass.ds(b, 1)].rearrange("o (t p) d -> p (o t) d", p=P),
                              xbatch(b).rearrange("p (t d) -> p t d", d=D)).then_inc(s_out, 16)
            act.wait_ge(s_out, 16 * NB)

        @block.tensor
        def _(pe):
            pe.wait_ge(s_c, 16 * 16)
            nc.tensor.transpose(ps[:, 6, 0:P], Wf[:, :], idf[:, :])
            nc.tensor.matmul(ps[:, 7, 0:2], Wf[:, :], acol[:, :], start=True, stop=True).then_inc(s_p, 1)

            def graph_t(S, i, evacuated):
                for j in range(2):
                    b = 2 * i + j
                    pe.wait_ge(S["xn"], b + 1)
                    wait(pe, S["lo"], b - 1)
                    if j == 0:
                        wait(pe, evacuated, 2 * i - 2)
                        if S is C:
                            wait(pe, C["fin"], 8 * i)
                    for t in range(T):
                        last = nc.tensor.transpose(ps[:, (0, 6)[j], t * P:(t + 1) * P], xn[j][:, t * D:(t + 1) * D],
                                                   idf[:, :])
                    last.then_inc(S["tr"], 1)

            def route_t(l, p, S, w=0):
                pe.wait_ge(R[l]["rows"], p + 1)
                pe.wait_ge(S["lo"], min(2 * p + 4, NB) if isinstance(p, int) else 2 * p + 4)
                for j in range(2):
                    v = bank((0, 6)[j]).bitcast(F16)
                    for t in range(T):
                        for part_ in range(2):
                            o = (t * 2 + part_) * P
                            src = (j * T + t) * ROW + part_ * D
                            last = nc.tensor.transpose(v[:, o:o + P], rows[w][:, src:src + D], idh[:, :])
                    last.then_inc(R[l]["t"], 1)

            def route_scores(l, p):
                pe.wait_ge(R[l]["x"], 2 * p + 2)
                wait(pe, R[l]["pos"], p)
                for t in range(TP):
                    o = ps[:, 1, t * E:(t + 1) * E]
                    xh, xl = xTr[:, 2 * t * P:(2 * t + 1) * P], xTr[:, (2 * t + 1) * P:(2 * t + 2) * P]
                    nc.tensor.matmul(o, xh, wR[l][0][:, :], start=True, stop=False)
                    nc.tensor.matmul(o, xh, wR[l][1][:, :], start=False, stop=False)
                    last = nc.tensor.matmul(o, xl, wR[l][0][:, :], start=False, stop=True)
                last.then_inc(R[l]["lg"], 1)

            def route_prefix(l, p):
                pe.wait_ge(R[l]["mk"], p + 1)
                for t in range(TP):
                    o = ps[:, 1, (TP + t) * E:(TP + t + 1) * E]
                    nc.tensor.matmul(o, low[:, P:2 * P], run[l][:, :], start=True, stop=False)
                    for s in range(t):
                        nc.tensor.matmul(o, low[:, P:2 * P], mk[:, s * E:(s + 1) * E], start=False, stop=False)
                    last = nc.tensor.matmul(o, low[:, 0:P], mk[:, t * E:(t + 1) * E], start=False, stop=True)
                last.then_inc(R[l]["pf"], 1)

            def count(l):
                pe.wait_ge(R[l]["pos"], NP)
                pe.wait_ge(R[l]["cnt"], NP)
                nc.tensor.matmul(ps[:, 1, 0:E], low[:, P:2 * P], run[l][:, :], start=True, stop=True).then_inc(R[l]["pf"], 1)

            def project_a(b, j):
                pe.wait_ge(A["lo"], b + 1)
                wait(pe, A["upd"], b)
                for t in range(T):
                    o = ps[:, 2 + t // 2, (t % 2) * 256:(t % 2) * 256 + 256]
                    xh, xl = xTh[j][:, t * P:(t + 1) * P], xTl[j][:, t * P:(t + 1) * P]
                    nc.tensor.matmul(o, xh, wA[0][:, :], start=True, stop=False)
                    nc.tensor.matmul(o, xh, wA[1][:, :], start=False, stop=False)
                    last = nc.tensor.matmul(o, xl, wA[0][:, :], start=False, stop=True)
                last.then_inc(A["proj"], 1)

            def aggregate(b, j):
                pe.wait_ge(A["upd"], b + 1)
                pe.wait_ge(A["conv"], b + 1)
                wait(pe, A["read"], b)
                for q in range(T):
                    o = ps[:, 4 + q // 2, (q % 2) * 256:(q % 2) * 256 + D + 1]
                    for t in range(T):
                        lhs = adjF[j][:, t * N + q * P:t * N + q * P + P]
                        nc.tensor.matmul(o, lhs, hh[j][:, t * (D + 1):(t + 1) * (D + 1)], start=(t == 0), stop=False)
                        last = nc.tensor.matmul(o[:, 0:D], lhs, hl[j][:, t * D:(t + 1) * D], start=False, stop=(t == T - 1))
                last.then_inc(A["agg"], 1)

            def body_a(i, p, w):
                if i is not None:
                    project_a(2 * i, 0)
                    project_a(2 * i + 1, 1)
                    aggregate(2 * i, 0)
                if p is not None:
                    route_t(0, p, A, w)
                    route_scores(0, p)
                if i is not None:
                    aggregate(2 * i + 1, 1)
                if p is not None:
                    route_prefix(0, p)
                if more(i):
                    graph_t(A, i + 1, R[0]["x"])

            pe.wait_ge(s_q, 1)
            graph_t(A, 0, R[0]["x"])
            pairs_by_two(pe, body_a)
            count(0)
            pe.wait_ge(s_w[0], 16 * 14)
            for e in range(E):
                for c in range(4):
                    last = nc.tensor.matmul(ps[:, 2, e * 4 + c:e * 4 + c + 1], stage[:, e * 512 + c * P:e * 512 + c * P + P],
                                            bT[:, e:e + 1], start=True, stop=True)
            last.then_inc(s_p, 1)

            def experts(l):
                S, nc_, hw = M[l], NC[l], HID[l]

                def turn(n, k4):
                    pe.wait_ge(S[f"ld{k4}"], rounds(n, k4) * 16 + 16)
                    wait(pe, S["xg"], n)
                    v = bank(6).bitcast(F16)
                    for part_ in range(2):
                        for h in range(H):
                            o = (part_ * H + h) * P
                            last = nc.tensor.transpose(v[:, o:o + P], gx[k4][:, h * ROW + part_ * D:h * ROW + part_ * D + D],
                                                       idh[:, :])
                    last.then_inc(S["t"], 1)

                def expert_of(n):
                    return pe.value_load(tab[l][0:1, bass.ds(n + NQ, 1)], min_val=0, max_val=E - 1)

                def up(n, k4, c, e):
                    k, q = k4 % 2, (nc_ * k4 + c) % 4
                    if c == 0:
                        pe.wait_ge(S["xg"], n + 1)
                    wait(pe, S["gelu"], nc_ * n + c - 3)
                    wh = wx[l][:, bass.ds(e * (4 * hw) + c * P, P)]
                    wl = wx[l][:, bass.ds(e * (4 * hw) + hw + c * P, P)]
                    nc.tensor.matmul(bank(q), wh, xg[k][:, 0:G], start=True, stop=False)
                    nc.tensor.matmul(bank(q), wh, xg[k][:, G:2 * G], start=False, stop=False)
                    nc.tensor.matmul(bank(q), wl, xg[k][:, 0:G], start=False, stop=True).then_inc(S["up"], 1)

                def down(n, k4, c, e):
                    k = k4 % 2
                    pe.wait_ge(S["lo"], nc_ * n + c + 1)
                    if c == 0:
                        wait(pe, S["yt"], n - 1)
                    wh = wx[l][:, bass.ds(e * (4 * hw) + 2 * hw + c * P, P)]
                    wl = wx[l][:, bass.ds(e * (4 * hw) + 3 * hw + c * P, P)]
                    nc.tensor.matmul(bank(4 + k), wh, hhi[k][:, c * G:(c + 1) * G], start=(c == 0), stop=False)
                    nc.tensor.matmul(bank(4 + k), wh, hlo[k][:, c * G:(c + 1) * G], start=False, stop=False)
                    last = nc.tensor.matmul(bank(4 + k), wl, hhi[k][:, c * G:(c + 1) * G], start=False, stop=(c == nc_ - 1))
                    if c == nc_ - 1:
                        last.then_inc(S["y"], 1)

                def turn_back(n, k):
                    pe.wait_ge(S["yt"], n + 1)
                    wait(pe, S["yr"], n)
                    for h in range(H):
                        last = nc.tensor.transpose(ps[:, 7, h * P:(h + 1) * P], yT[k][:, h * P:(h + 1) * P], idf[:, :])
                    last.then_inc(S["ytt"], 1)

                pe.wait_ge(R[l]["tab"], 1)
                pe.wait_ge(WP[l]["lo"], E)
                turn(0, 0)
                turn(1, 1)
                e0 = expert_of(0)
                for c in range(nc_):
                    up(0, 0, c, e0)

                def body(n, k4):
                    now, then = expert_of(n), expert_of(n + 1)
                    if not (isinstance(n, int) and n + 2 >= NQ):
                        turn(n + 2, (k4 + 2) % 4)
                    for c in range(nc_):
                        up(n + 1, (k4 + 1) % 4, c, then)
                        if c == nc_ // 2 and not (isinstance(n, int) and n == 0):
                            turn_back(n - 1, 1 - k4 % 2)
                        down(n, k4, c, now)

                groups(pe, body)
                turn_back(NQ - 2, NQ % 2)
                e1 = expert_of(NQ - 1)
                for c in range(nc_):
                    down(NQ - 1, (NQ - 1) % 4, c, e1)
                turn_back(NQ - 1, (NQ - 1) % 2)

            experts(0)

            def project_c(b, j):
                pe.wait_ge(C["lo"], b + 1)
                wait(pe, C["bias"], b)
                for t in range(T):
                    o = ps[:, 2 + t // 2, (t % 2) * 256:(t % 2) * 256 + D + 2]
                    xh, xl = xTh[j][:, t * P:(t + 1) * P], xTl[j][:, t * P:(t + 1) * P]
                    nc.tensor.matmul(o, xh, wC[0][:, :], start=True, stop=False)
                    nc.tensor.matmul(o, xh, wC[1][:, :], start=False, stop=False)
                    nc.tensor.matmul(o, xl, wC[0][:, :], start=False, stop=True)
                nc.tensor.matmul(bank(7), wS[0][:, :], xTh[j][:, :], start=True, stop=False)
                nc.tensor.matmul(bank(7), wS[0][:, :], xTl[j][:, :], start=False, stop=False)
                nc.tensor.matmul(bank(7), wS[1][:, :], xTh[j][:, :], start=False, stop=True).then_inc(C["proj"], 1)

            def turn_p(b, t):
                q = 4 * b + t
                pe.wait_ge(C["p"], q + 1)
                wait(pe, C["pt"], q - 1)
                for c in range(T):
                    last = nc.tensor.transpose(ps[:, 4 + t % 2, c * P:(c + 1) * P], part(2, t)[:, c * P:(c + 1) * P],
                                               idf[:, :])
                last.then_inc(C["ptr"], 1)

            def times(b, j, t):
                q = 4 * b + t
                pe.wait_ge(C["pt"], q + 1)
                pe.wait_ge(C["wh"], b + 1)
                wait(pe, C["fin"], q - 1)
                for c in range(T):
                    last = nc.tensor.matmul(ps[:, av_bank(t), 0:D + 1], part(3, t)[:, c * P:(c + 1) * P],
                                            whE[j][:, c * (D + 1):(c + 1) * (D + 1)], start=(c == 0), stop=(c == T - 1))
                last.then_inc(C["av"], 1)

            def attend(i):
                for q in range(2 * T):
                    turn_p(2 * i + q // T, q % T)
                    if q >= 2:
                        times(2 * i + (q - 2) // T, (q - 2) // T, (q - 2) % T)
                times(2 * i + 1, 1, T - 2)
                times(2 * i + 1, 1, T - 1)

            def body_c(i, p):
                if i is not None:
                    project_c(2 * i, 0)
                if p is not None:
                    route_t(1, p, C)
                    route_scores(1, p)
                if i is not None:
                    project_c(2 * i + 1, 1)
                if p is not None:
                    route_prefix(1, p)
                if i is not None:
                    attend(i)
                if more(i):
                    graph_t(C, i + 1, R[1]["x"])

            graph_t(C, 0, R[1]["x"])
            pairs_of(pe, body_c, ahead=1)
            count(1)
            experts(1)

        @block.vector
        def _(dve):
            ch = Chain(dve, s_ch)
            nc.vector.memset(zt[:, 63:64], 0.0)
            for j in range(2):
                nc.vector.memset(v3(hh[j][:, :], D + 1)[:, :, D:D + 1], 1.0)
                nc.vector.memset(v3(whE[j][:, :], D + 1)[:, :, D:D + 1], 1.0)
                nc.vector.memset(run[j][:, :], 0.0)
            for w in range(2):
                nc.vector.memset(rows[w][:, :].bitcast(U32), 0)
            ch(nc.vector.memset(padr[:, :].bitcast(U32), 0))
            nc.vector.memset(padr[:, :].bitcast(U32).rearrange("p (h r) -> p h r", h=H)[:, :, D:D + 1], NOWHERE).then_inc(s_m, 1)

            def split(hi, lo, src):
                ch(nc.vector.tensor_copy(hi, src))
                nc.vector.tensor_tensor(lo, src, hi, ALU.subtract)

            def sums_of(n0, tiles):
                for t in tiles:
                    last = nc.vector.bn_stats(st6[:, 6 * t:6 * t + 6], xtile(n0 + t))
                return last

            def statistics(mvx, n0, tiles=range(TP)):
                ch(sums_of(n0, tiles), wait_alone)
                for t in range(TP):
                    last = nc.vector.bn_aggr(mvx[:, 2 * t:2 * t + 2], st6[:, 6 * t:6 * t + 6])
                ch(last)

            def graph_statistics(S, i, tiles=range(TP)):
                statistics(mvc, i * TP, tiles)
                nc.vector.tensor_scalar(col(uc[:, :]), v3(mvc[:, :], 2)[:, :, 1:2], EPS, None, ALU.add).then_inc(S["u"], 1)

            def graph_shift(S, i):
                dve.wait_ge(S["r"], i + 1)
                nc.vector.scalar_tensor_tensor(col(nm[:, :]), v3(mvc[:, :], 2)[:, :, 0:1], -1.0, col(rc[:, :]),
                                               ALU.mult, ALU.mult).then_inc(S["nm"], 1)

            dve.wait_ge(s_x[0], 16)
            graph_statistics(A, 0)
            dve.wait_ge(s_c, 16 * 16)
            split(wA[0][:, :], wA[1][:, :], smf[:, 0:2 * D])
            for l in range(2):
                split(wR[l][0][:, :], wR[l][1][:, :], smf[:, 2 * D + 8 * l:2 * D + 8 * l + 8])
            dve.wait_ge(s_p, 1)
            ch(nc.vector.tensor_copy(wcf[:, 0:D], ps[:, 6, 0:P]))
            ch(nc.vector.tensor_copy(wcf[:, D:D + 2], ps[:, 7, 0:2]))
            split(wC[0][:, :], wC[1][:, :], wcf[:, :])
            ch(mark(nc.vector))
            for k in range(2):
                last = nc.vector.tensor_copy(wS[k][:, :], wC[k][:, D + 1:D + 2].to_broadcast([P, P]))
            ch(last)
            mark(nc.vector).then_inc(s_q, 1)
            def lo_part(S, i):
                for j in range(2):
                    b = 2 * i + j
                    dve.wait_ge(S["hi"], b + 1)
                    wait(dve, S["proj"], b - 1)
                    nc.vector.tensor_tensor(xTl[j][:, :], bank((0, 6)[j]), xTh[j][:, :], ALU.subtract).then_inc(S["lo"], 1)

            def route_stats(l, p):
                statistics(mvr, p * TP)
                v = col(mvr[:, :].rearrange("p (t two) -> p two t", two=2)[:, 1, :])
                if l == 0:
                    nc.vector.tensor_scalar(col(ur[:, 0:TP]), v, 1.0 + EPS, EPS * EPS, ALU.mult, ALU.add)
                    nc.vector.tensor_scalar(col(ur[:, TP:2 * TP]), v, EPS, None, ALU.add).then_inc(R[l]["u"], 1)
                else:
                    nc.vector.tensor_scalar(col(ur[:, 0:TP]), v, EPS, None, ALU.add).then_inc(R[l]["u"], 1)

            def route_norm(l, p):
                dve.wait_ge(R[l]["r"], p + 1)
                if l == 0:
                    ch(nc.vector.tensor_tensor(cinv[:, :], ur[:, 0:TP], rr[:, 0:TP], ALU.mult))
                    ch(nc.vector.tensor_tensor(cinv[:, :], cinv[:, :], rr[:, TP:2 * TP], ALU.mult))
                for t in range(TP):
                    last = nc.vector.tensor_scalar(xr[:, t * D:(t + 1) * D], xtile(p * TP + t), mvr[:, 2 * t:2 * t + 1],
                                                   rr[:, t:t + 1], ALU.subtract, ALU.mult)
                last.then_inc(R[l]["xr"], 1)

            def route_rows(l, p, w=0):
                dve.wait_ge(R[l]["hi"], p + 1)
                nc.vector.tensor_tensor(rows_of(w, 0, D, 2 * D), v3(xr[:, :], D), rows_of(w, 0, 0, D), ALU.subtract)
                last = nc.vector.tensor_copy(rows[w][:, :].bitcast(U32).rearrange("p (n r) -> p n r", r=ROW // 2)[:, :, D:D + 1],
                                             col(idt[:, bass.ds(p * (K * TP), K * TP)]))
                if l == 1:
                    ch(last)
                    last = nc.vector.tensor_copy(rows_of(w, 1, 0, 2 * D), rows_of(w, 0, 0, 2 * D))
                last.then_inc(R[l]["rows"], 1)

            def bcast(ap, n):
                return ap.to_broadcast([P, n, E])

            def route_choose(l, p):
                dve.wait_ge(R[l]["lg"], p + 1)
                sc = v3(ps[:, 1, 0:TP * E], E)
                rbv = rb[l][:, :].rearrange("p (o e) -> p o e", o=1).to_broadcast([P, TP, E])
                if l == 0:
                    ch(nc.vector.tensor_tensor(v3(lg[:, :], E), sc, bcast(col(cinv[:, :]), TP), ALU.mult))
                    ch(nc.vector.tensor_tensor(v3(lg[:, :], E), v3(lg[:, :], E), rbv, ALU.add), wait_alone)
                else:
                    ch(nc.vector.tensor_tensor(v3(lg[:, :], E), sc, rbv, ALU.add), wait_alone)
                for t in range(TP):
                    last = nc.vector.max(mx8[:, t * E:(t + 1) * E], lg[:, t * E:(t + 1) * E])
                ch(last, wait_alone)
                for t in range(TP):
                    last = nc.vector.max_index(ix8[:, t * E:(t + 1) * E], mx8[:, t * E:(t + 1) * E], lg[:, t * E:(t + 1) * E])
                ch(last)
                if l == 0:
                    nc.vector.tensor_tensor(col(dd[:, 0:TP]), v3(mx8[:, :], E)[:, :, 0:1], v3(mx8[:, :], E)[:, :, 1:2],
                                            ALU.subtract).then_inc(R[0]["d"], 1)
                ch(nc.vector.tensor_copy(ixf[:, :], ix8[:, :]))
                for k in range(K):
                    last = nc.vector.tensor_tensor(v3(oh[k][:, :], E), v3(io8[:, :], E),
                                                   bcast(v3(ixf[:, :], E)[:, :, k:k + 1], TP), ALU.is_equal)
                ch(last)
                nc.vector.tensor_tensor(mk[:, :], oh[0][:, :], oh[1][:, :], ALU.add).then_inc(R[l]["mk"], 1)

            def route_places(l, p, w=0):
                dve.wait_ge(R[l]["pf"], p + 1)
                ch(nc.vector.tensor_tensor(pos[:, :], ps[:, 1, TP * E:2 * TP * E], ebase[:, :], ALU.add))
                for k in range(K):
                    ch(nc.vector.tensor_tensor(tm8[:, :], pos[:, :], oh[k][:, :], ALU.mult))
                    ch(nc.vector.reduce_sum(posf[:, k * TP:(k + 1) * TP], v3(tm8[:, :], E), axis=AX.X))
                if l == 0:
                    dve.wait_ge(R[0]["th"], p + 1)
                    for k in range(K):
                        wt = rows[w][:, k * TP * ROW:(k + 1) * TP * ROW].bitcast(F32).rearrange("p (t r) -> p t r", t=TP)
                        nc.vector.tensor_scalar(wt[:, :, D + 1:D + 2], col(dd[:, TP:2 * TP]), (0.5, -0.5)[k], 0.5,
                                                ALU.mult, ALU.add)
                nc.vector.tensor_copy(posi[w][:, :], posf[:, :]).then_inc(R[l]["pos"], 1)
                ch(nc.vector.reduce_sum(cnt[:, :], mk[:, :].rearrange("p (t e) -> p e t", e=E), axis=AX.X))
                nc.vector.tensor_tensor(run[l][:, :], run[l][:, :], cnt[:, :], ALU.add).then_inc(R[l]["cnt"], 1)

            def table(l):
                F = [tf[:, k * E:(k + 1) * E] for k in range(8)]
                nf, padf, tg, c1, c2, c3 = F[0], F[1], F[2], F[3], F[4], F[5]
                dve.wait_ge(R[l]["pf"], NP + 1)
                ch(nc.vector.tensor_copy(nf, ps[0:1, 1, 0:E]))
                ch(nc.vector.tensor_tensor(padf, nf, ebase[0:1, 0:E], ALU.add))
                ch(nc.vector.tensor_copy(tab[l][:, 2 * NQ:2 * NQ + E], padf))
                ch(nc.vector.tensor_scalar(nf, nf, float(G - 1), None, ALU.add))
                ch(nc.vector.tensor_copy(ti[:, :], nf))
                ch(nc.vector.tensor_scalar(ti[:, :], ti[:, :], G.bit_length() - 1, None, ALU.arith_shift_right))
                ch(nc.vector.tensor_copy(tg, ti[:, :]))
                prev = tg
                for s, nxt in ((1, c1), (2, c2), (4, c3)):
                    ch(nc.vector.tensor_copy(nxt[:, 0:s], prev[:, 0:s]))
                    ch(nc.vector.tensor_tensor(nxt[:, s:E], prev[:, s:E], prev[:, 0:E - s], ALU.add))
                    prev = nxt
                done = tq[:, 0:NQ * E].rearrange("p (q e) -> p q e", e=E)
                past = tq[:, NQ * E:2 * NQ * E].rearrange("p (q e) -> p q e", e=E)

                def over(ap):
                    return ap.rearrange("p (o e) -> p o e", o=1).to_broadcast([1, NQ, E])

                ch(nc.vector.tensor_tensor(done, over(prev), ioq[:, :].rearrange("p (q e) -> p q e", e=E), ALU.is_le))
                ch(nc.vector.tensor_tensor(past, done, over(tg), ALU.mult))
                eq, st, us, of = [tr[:, k * NQ:(k + 1) * NQ] for k in range(4)]
                ch(nc.vector.reduce_sum(eq, done, axis=AX.X))
                ch(nc.vector.reduce_sum(st, past, axis=AX.X))
                ch(nc.vector.tensor_tensor(st.rearrange("p (q o) -> p q o", o=1),
                                           ioq[:, :].rearrange("p (q e) -> p q e", e=E)[:, :, 0:1],
                                           st.rearrange("p (q o) -> p q o", o=1), ALU.subtract))
                ch(nc.vector.tensor_scalar(us, eq, float(E), float(G), ALU.is_lt, ALU.mult))
                ch(nc.vector.tensor_tensor(st, st, us, ALU.mult))
                ch(nc.vector.tensor_scalar(of, eq, float(CAP), None, ALU.mult))
                ch(nc.vector.tensor_tensor(of, of, st, ALU.add))
                ch(nc.vector.tensor_copy(tab[l][:, 0:NQ], of))
                ch(nc.vector.tensor_scalar(eq, eq, float(E - 1), None, ALU.min))
                nc.vector.tensor_copy(tab[l][:, NQ:2 * NQ], eq).then_inc(R[l]["tab"], 1)

            def weights_lo(l, e):
                dve.wait_ge(WP[l]["hi"], e + 1)
                for src, factor, (hi, lo) in weight_parts(l, e):
                    last = nc.vector.scalar_tensor_tensor(lo, src, factor, hi, ALU.mult, ALU.subtract)
                last.then_inc(WP[l]["lo"], 1)

            def a_parts(b, j):
                dve.wait_ge(A["hh"], b + 1)
                wait(dve, A["agg"], b - 1)
                pv = ps[:, 2:4, :].rearrange("p k (h d) -> p (k h) d", h=2)
                nc.vector.tensor_tensor(v3(hl[j][:, :], D), pv[:, :, 0:D], v3(hh[j][:, :], D + 1)[:, :, 0:D], ALU.subtract)
                nc.vector.tensor_tensor(v3(upd[j][:, :], D), pv[:, :, D:2 * D],
                                        gb[:, :].rearrange("p (o d) -> p o d", o=1).to_broadcast([P, T, D]),
                                        ALU.add).then_inc(A["upd"], 1)

            def a_sum(b, j):
                dve.wait_ge(A["agg"], b + 1)
                av = ps[:, 4:6, :].rearrange("p k (h d) -> p (k h) d", h=2)
                ch(nc.vector.tensor_scalar(col(deg[j][:, 0:T]), av[:, :, D:D + 1], 1.0, None, ALU.max))
                ch(nc.vector.reciprocal(deg[j][:, T:2 * T], deg[j][:, 0:T]))
                for t in range(T):
                    last = nc.vector.scalar_tensor_tensor(upd[j][:, t * D:(t + 1) * D], av[:, t, 0:D],
                                                          deg[j][:, T + t:T + t + 1], upd[j][:, t * D:(t + 1) * D],
                                                          ALU.mult, ALU.add)
                last.then_inc(A["read"], 1)
                dve.wait_ge(A["read"], b + 1)
                ch(nc.vector.scalar_tensor_tensor(xbatch(b), upd[j][:, :], 0.0, xbatch(b), ALU.max, ALU.add), wait_alone)

            def body_a(i, p, w):
                if i is not None:
                    a_parts(2 * i, 0)
                if p is not None:
                    if isinstance(p, int) and p == 0:
                        dve.wait_ge(s_w[0], 16 * 14)
                        nc.vector.tensor_scalar(g64[:, :], gT[:, :], WS, None, ALU.mult).then_inc(WP[0]["g"], 1)
                        dve.wait_ge(WP[0]["g"], 1)
                    route_norm(0, p)
                if i is not None:
                    a_parts(2 * i + 1, 1)
                if p is not None:
                    route_rows(0, p, w)
                if i is not None:
                    a_sum(2 * i, 0)
                    if isinstance(i, int) and i == 1:
                        for q in range(1, 4):
                            dve.wait_ge(s_x[q], 16)
                if more(i):
                    graph_statistics(A, i + 1)
                if p is not None:
                    route_choose(0, p)
                if i is not None:
                    a_sum(2 * i + 1, 1)
                if more(i):
                    graph_shift(A, i + 1)
                if p is not None:
                    route_places(0, p, w)
                if i is not None:
                    route_stats(0, i)
                if p is not None:
                    weights_lo(0, p)
                if more(i):
                    lo_part(A, i + 1)

            graph_shift(A, 0)
            lo_part(A, 0)
            pairs_by_two(dve, body_a, ch, 48)
            table(0)

            dve.wait_ge(s_p, 2)
            bv = bx[0][:, :].rearrange("p (e c) -> p e c", c=NC[0] + 1)[:, :, 0:NC[0]]
            nc.vector.tensor_tensor(bv, bv, v3(ps[:, 2, 0:E * NC[0]], NC[0]), ALU.add).then_inc(s_q, 1)

            def experts(l, steps):
                S, nc_ = M[l], NC[l]

                def take(n, k4):
                    dve.wait_ge(S["t"], n + 1)
                    wait(dve, S["yr"], n - 3)
                    nc.vector.tensor_copy(v3(idg[k4][:, :], 2),
                                          gx[k4][:, :].bitcast(U32).rearrange("p (h r) -> p h r", h=H)[:, :, D:D + 2])
                    wait(dve, S["up"], nc_ * (n - 1))
                    nc.vector.tensor_copy(xg[k4 % 2][:, :], bank(6).bitcast(F16)).then_inc(S["xg"], 1)

                def hidden(n, k4, c):
                    k, q = k4 % 2, (nc_ * k4 + c) % 4
                    dve.wait_ge(S["gelu"], nc_ * n + c + 1)
                    if c == 0:
                        wait(dve, S["y"], n - 1)
                    hi = hhi[k][:, c * G:(c + 1) * G]
                    ch(nc.vector.tensor_copy(hi, hbuf(q)))
                    nc.vector.tensor_tensor(hlo[k][:, c * G:(c + 1) * G], hbuf(q), hi, ALU.subtract).then_inc(S["lo"], 1)

                def result(n, k4):
                    dve.wait_ge(S["ytt"], n + 1)
                    wait(dve, S[f"sc{k4}"], 16 * H * rounds(n, k4))
                    dve.wait_ge(S["xg"], n + 1)
                    nc.vector.tensor_copy(col(idc[k4][:, :]), v3(idg[k4][:, :], 2)[:, :, 0:1])
                    if l == 0:
                        for h in range(H):
                            last = nc.vector.tensor_scalar(yrow[k4][:, h * D:(h + 1) * D], ps[:, 7, h * D:(h + 1) * D],
                                                           idg[k4][:, 2 * h + 1:2 * h + 2].bitcast(F32), None, ALU.mult)
                    else:
                        last = nc.vector.tensor_copy(yrow[k4][:, :], bank(7))
                    last.then_inc(S["yr"], 1)

                take(0, 0)
                take(1, 1)
                for c in range(nc_):
                    hidden(0, 0, c)

                def body(n, k4):
                    if not (isinstance(n, int) and n + 2 >= NQ):
                        take(n + 2, (k4 + 2) % 4)
                    for c in range(nc_):
                        hidden(n + 1, (k4 + 1) % 4, c)
                        if c == nc_ // 2 - 1 and not (isinstance(n, int) and n == 0):
                            result(n - 1, (k4 + 3) % 4)

                groups(dve, body, ch, steps, (lambda e: weights_lo(1, e)) if l == 0 else None)
                result(NQ - 2, (NQ - 2) % 4)
                result(NQ - 1, (NQ - 1) % 4)

            experts(0, 4 * NC[0])
            def c_combine(i, j, k):
                b = 2 * i + j
                if k == 0:
                    dve.wait_ge(C[f"y{j}"], 16 * K * (i + 1))
                else:
                    wait_alone(dve, (C["comb"], b * K + 1))
                nc.vector.tensor_tensor(xbatch(b), xbatch(b), yb[j][:, k * N:(k + 1) * N], ALU.add).then_inc(C["comb"], 1)

            def c_statistics(i, j):
                wait_alone(dve, (C["comb"], K * (2 * i + j + 1)))
                if j == 0:
                    sums_of(i * TP, range(T))
                else:
                    graph_statistics(C, i, range(T, TP))

            def c_sums(b, j, t):
                if t == 0:
                    wait_alone(dve, (C["proj"], b + 1), (C["conv"], b + 1))
                last = nc.vector.tensor_tensor_reduce(
                    out=tt(j, t), in0=bank(7), in1=adjF[j][:, t * N:(t + 1) * N].bitcast(BF16), scale=1.0,
                    scalar=-3.0e38, op0=ALU.add, op1=ALU.max, accum_out=rowb[j][:, 2 * T + t:2 * T + t + 1])
                if t == T - 1:
                    last.then_inc(C["sum"], 1)

            def c_bias(b, j):
                r_ = rowb[j]
                M_, s1, m_ = r_[:, 2 * T:3 * T], r_[:, 3 * T:4 * T], r_[:, 4 * T:5 * T]
                dve.wait_ge(C["sum"], b + 1)
                dve.wait_ge(C["wh"], b + 1)
                sv = ps[:, 2:4, :].rearrange("p k (h d) -> p (k h) d", h=2)
                ch(nc.vector.tensor_copy(col(s1), sv[:, :, D:D + 1]))
                ch(nc.vector.tensor_tensor(M_, M_, s1, ALU.add))
                ch(nc.vector.scalar_tensor_tensor(m_, M_, SLOPE, M_, ALU.mult, ALU.max))
                nc.vector.tensor_tensor(r_[:, 0:T], s1, m_, ALU.subtract)
                nc.vector.scalar_tensor_tensor(r_[:, T:2 * T], s1, SLOPE, m_, ALU.mult, ALU.subtract).then_inc(C["bias"], 1)

            def take_max(b, t):
                q = 4 * b + t
                dve.wait_ge(C["e"], q + 1)
                wait(dve, C["ptr"], q - 1)
                nc.vector.tensor_tensor(part(2, t), part(0, t), part(1, t), ALU.max).then_inc(C["p"], 1)

            def divide(b, j, t):
                dve.wait_ge(C["av"], 4 * b + t + 1)
                rec = rowb[j][:, 5 * T + t:5 * T + t + 1]
                ch(nc.vector.reciprocal(rec, ps[:, av_bank(t), D:D + 1]))
                nc.vector.tensor_scalar(hpb[j][:, t * D:(t + 1) * D], ps[:, av_bank(t), 0:D], rec, None, ALU.mult
                                        ).then_inc(C["fin"], 1)

            def c_add(b, j):
                dve.wait_ge(C["fin"], 4 * b + 4)
                ch(nc.vector.scalar_tensor_tensor(xbatch(b), hpb[j][:, :], 0.0, xbatch(b), ALU.max, ALU.add))
                dve.wait_ge(C["ex"], b + 1)
                ch(nc.vector.scalar_tensor_tensor(xbatch(b), mnb[j][:, :], -1.0, xbatch(b), ALU.add, ALU.add), wait_alone)

            def body_c(i, p):
                if p is not None:
                    route_norm(1, p)
                if i is not None:
                    c_sums(2 * i, 0, 0)
                    c_sums(2 * i, 0, 1)
                if p is not None:
                    route_rows(1, p)
                if i is not None:
                    c_sums(2 * i, 0, 2)
                    c_sums(2 * i, 0, 3)
                    c_bias(2 * i, 0)
                if more(i):
                    c_combine(i + 1, 0, 0)
                    c_combine(i + 1, 0, 1)
                if p is not None:
                    route_choose(1, p)
                if i is None:
                    route_places(1, p)
                    return
                for q in range(2 * T):
                    take_max(2 * i + q // T, q % T)
                    if q < 2:
                        c_sums(2 * i + 1, 1, 2 * q)
                        c_sums(2 * i + 1, 1, 2 * q + 1)
                    if q == 2:
                        c_bias(2 * i + 1, 1)
                        if more(i):
                            c_statistics(i + 1, 0)
                    if q == 3 and p is not None:
                        route_places(1, p)
                    if q in (4, 5) and more(i):
                        c_combine(i + 1, 1, q - 4)
                    if q == 6 and more(i):
                        c_statistics(i + 1, 1)
                    if q >= 3:
                        divide(2 * i + (q - 3) // T, (q - 3) // T, (q - 3) % T)
                divide(2 * i + 1, 1, T - 3)
                divide(2 * i + 1, 1, T - 2)
                if more(i):
                    graph_shift(C, i + 1)
                c_add(2 * i, 0)
                divide(2 * i + 1, 1, T - 1)
                c_add(2 * i + 1, 1)
                route_stats(1, i)
                if more(i):
                    lo_part(C, i + 1)

            for j in range(2):
                for k in range(K):
                    c_combine(0, j, k)
            c_statistics(0, 0)
            c_statistics(0, 1)
            graph_shift(C, 0)
            lo_part(C, 0)
            pairs_of(dve, body_c, ch, 34, ahead=1)
            table(1)
            experts(1, 4 * NC[1])

            with dve.Fori(0, NB // 4) as i:
                for m in range(4):
                    b = 4 * i + m
                    dve.wait_ge(Z[f"y{m}"], 16 * K * (i + 1))
                    nc.vector.tensor_tensor(xbatch(b), xbatch(b), zb(m)[:, 0:N], ALU.add).then_inc(Z["add"], 1)
                    dve.wait_ge(Z["add"], K * b + 1)
                    nc.vector.tensor_tensor(xbatch(b), xbatch(b), zb(m)[:, N:2 * N], ALU.add).then_inc(Z["add"], 1)


_INS = ['x', 'adj', 'L0_gnn_W_msg', 'L0_gnn_W_upd', 'L0_gnn_bias', 'L0_ffn_Wr', 'L0_ffn_br', 'L0_ffn_ln_g', 'L0_ffn_ln_b',
        'L0_ffn_W1', 'L0_ffn_b1', 'L0_ffn_W2', 'L0_ffn_b2', 'L1_gnn_W', 'L1_gnn_a', 'L1_ffn_Wg', 'L1_ffn_bg', 'L1_ffn_W1',
        'L1_ffn_b1', 'L1_ffn_W2', 'L1_ffn_b2']


def kernel(**inputs):
    import concourse.bacc as _bacc
    from concourse.bass_utils import run_bass_kernel_spmd as _run

    nc = _bacc.Bacc("TRN2", target_bir_lowering=False, num_devices=1)
    arrays, args = {}, []

    def give(name, a):
        arrays[name] = a
        args.append(nc.dram_tensor(name, a.shape, mybir.dt.from_np(a.dtype), kind="ExternalInput").ap())

    for name in _INS:
        give(f"in_{name}_dram", np.ascontiguousarray(inputs[name]))
    give("c_identf", np.eye(P, dtype=np.float32))
    give("c_identh", np.eye(P, dtype=np.float16))
    give("c_lower", np.concatenate([np.triu(np.ones((P, P), np.float16), 1), np.ones((P, P), np.float16)], 1))
    e8 = np.tile(np.arange(E, dtype=np.float32), (P, TP))
    give("c_iota8", np.stack([e8, e8 * CAP]))
    k, i, t, p = np.meshgrid(np.arange(K), np.arange(NP), np.arange(TP), np.arange(P), indexing="ij")
    give("c_ids", np.ascontiguousarray((k * TOK + (i * TP + t) * P + p).transpose(3, 1, 0, 2).reshape(P, -1).astype(np.uint32)))
    give("c_iotaq", np.repeat(np.arange(NQ, dtype=np.float32), E)[None])
    args.append(nc.dram_tensor("out_0_dram", (NB, N, D), F32, kind="ExternalOutput").ap())
    build(nc, *args)
    r = _run(nc, [arrays], core_ids=[0])
    return r.results[0]["out_0_dram"]
```
